# Optimizing a Trainium2 kernel written in Bass

```python
import numpy as np
import jax
import jax.numpy as jnp

def _softmax(x, axis=-1):
    return jax.nn.softmax(x, axis=axis)

def _gelu(x):
    return jax.nn.gelu(x, approximate=True)

def _silu(x):
    return jax.nn.silu(x)

def _sigmoid(x):
    return jax.nn.sigmoid(x)

def _layernorm(x, axis=-1, eps=1e-05):
    m = jnp.mean(x, axis=axis, keepdims=True)
    v = jnp.var(x, axis=axis, keepdims=True)
    return (x - m) / jnp.sqrt(v + eps)

def _scatter_add(tgt, idx, src, axis=0):
    return tgt.at[idx].add(src)

def _segment_sum(src, seg, n):
    return jax.ops.segment_sum(src, seg, n)
kernel_name = 'mk_adaln_d1_jaxref_r2_28e614'

def setup_inputs(seed: int=0):
    np.random.seed(seed)
    _w = jnp.asarray

    def _L0_attn_setup():
        import jax, jax.numpy as jnp
        import numpy as np
        N_STATE = 64
        SEQ_L = 2048
        BATCH, HCH = (16, 256)
        DT_MIN, DT_MAX = (0.001, 0.1)

        def _make_DPLR_HiPPO(N):
            P = np.sqrt(1 + 2 * np.arange(N))
            A = P[:, None] * P[None, :]
            A = np.tril(A) - np.diag(np.arange(N))
            nhippo = -A
            p = 0.5 * np.sqrt(2 * np.arange(1, N + 1) + 1.0)
            q = 2 * p
            S = nhippo + p[:, None] * q[None, :]
            Lambda, V = np.linalg.eig(S)
            Vc = V.conj().T
            p_t = Vc @ p
            q_t = Vc @ q.conj()
            return (Lambda, p_t, q_t, Vc)

        def _ri(z):
            return np.stack([z.real, z.imag], axis=-1).astype(np.float32)

        def _cplx(x_ri):
            return x_ri[..., 0] + 1j * x_ri[..., 1]

        def _s4_kernel(Lambda, p, q, B, Ct, step, L):
            Omega = jnp.exp(-2j * jnp.pi * (jnp.arange(L) / L))
            g = 2.0 / step * ((1.0 - Omega) / (1.0 + Omega))
            c = 2.0 / (1.0 + Omega)
            denom = g[:, None] - Lambda[None, :]
            cauchy = lambda v: (v[None, :] / denom).sum(-1)
            k00 = cauchy(Ct.conj() * B)
            k01 = cauchy(Ct.conj() * p)
            k10 = cauchy(q.conj() * B)
            k11 = cauchy(q.conj() * p)
            at_roots = c * (k00 - k01 * (1.0 / (1.0 + k11)) * k10)
            return jnp.fft.ifft(at_roots, L).real
        key = jax.random.key(seed)
        k_u, k_ct, k_b, k_d, k_ls = jax.random.split(key, 5)
        Lambda, p, q, Vc = _make_DPLR_HiPPO(N_STATE)
        u = jax.random.normal(k_u, (BATCH, HCH, SEQ_L), dtype=jnp.float32)
        Ct_ri = jax.random.normal(k_ct, (1, N_STATE, 2), dtype=jnp.float32) / np.sqrt(N_STATE)
        Bp = jax.random.normal(k_b, (N_STATE, 1), dtype=jnp.float32) / np.sqrt(N_STATE)
        D = jax.random.uniform(k_d, (1,), dtype=jnp.float32)
        log_step = jax.random.uniform(k_ls, (1,), dtype=jnp.float32, minval=np.log(DT_MIN), maxval=np.log(DT_MAX))
        return {'u': u, 'Lambda_ri': jnp.asarray(_ri(Lambda)), 'p_ri': jnp.asarray(_ri(p)), 'q_ri': jnp.asarray(_ri(q)), 'Vc_ri': jnp.asarray(_ri(Vc)), 'Ct_ri': Ct_ri, 'Bp': Bp, 'D': D, 'log_step': log_step}
    _L0_attn_in = _L0_attn_setup()

    def _L0_ffn_setup():
        import jax, jax.numpy as jnp
        import numpy as np
        key = jax.random.key(seed)
        k = jax.random.split(key, 6)
        x = jax.random.normal(k[0], (4, 1024, 2048), jnp.float32)
        W = jax.random.normal(k[1], (2048, 2048), jnp.float32) * 0.02
        bias = jax.random.normal(k[2], (2048,), jnp.float32) * 0.02
        A = jax.random.normal(k[3], (16, 16, 2048), jnp.float32) * 0.02
        Bf = jax.random.normal(k[4], (16, 2048, 16), jnp.float32) * 0.02
        coeffs = jax.random.uniform(k[5], (16,), jnp.float32)
        scales = jnp.full((16,), 0.5, jnp.float32)
        return {'x': x, 'W': W, 'bias': bias, 'A': A, 'Bf': Bf, 'coeffs': coeffs, 'scales': scales}
    _L0_ffn_in = _L0_ffn_setup()
    _L0_c = _w((lambda *s: np.random.randn(*s).astype(np.float32) * 0.05)(4, 2048))
    _L0_wmod = _w((lambda *s: np.random.randn(*s).astype(np.float32) * 0.05)(2048, 6 * 2048) * 2048 ** (-0.5))
    _d = {'L0_attn_u': _L0_attn_in['u'], 'L0_attn_Lambda_ri': _L0_attn_in['Lambda_ri'], 'L0_attn_p_ri': _L0_attn_in['p_ri'], 'L0_attn_q_ri': _L0_attn_in['q_ri'], 'L0_attn_Vc_ri': _L0_attn_in['Vc_ri'], 'L0_attn_Ct_ri': _L0_attn_in['Ct_ri'], 'L0_attn_Bp': _L0_attn_in['Bp'], 'L0_attn_D': _L0_attn_in['D'], 'L0_attn_log_step': _L0_attn_in['log_step'], 'L0_ffn_W': _L0_ffn_in['W'], 'L0_ffn_bias': _L0_ffn_in['bias'], 'L0_ffn_A': _L0_ffn_in['A'], 'L0_ffn_Bf': _L0_ffn_in['Bf'], 'L0_ffn_coeffs': _L0_ffn_in['coeffs'], 'L0_ffn_scales': _L0_ffn_in['scales'], 'L0_c': _L0_c, 'L0_wmod': _L0_wmod}
    _x0 = _d['L0_attn_u']
    _d['L0_attn_u'] = jax.random.normal(jax.random.fold_in(jax.random.key(seed), 1), (4, 1024, 2048), dtype=_x0.dtype)
    del _x0
    return _d

def reference(L0_attn_u, L0_attn_Lambda_ri, L0_attn_p_ri, L0_attn_q_ri, L0_attn_Vc_ri, L0_attn_Ct_ri, L0_attn_Bp, L0_attn_D, L0_attn_log_step, L0_ffn_W, L0_ffn_bias, L0_ffn_A, L0_ffn_Bf, L0_ffn_coeffs, L0_ffn_scales, L0_c, L0_wmod):

    def _L0_attn_ref(u, Lambda_ri, p_ri, q_ri, Vc_ri, Ct_ri, Bp, D, log_step):
        import jax, jax.numpy as jnp
        import numpy as np
        N_STATE = 64
        SEQ_L = 2048
        BATCH, HCH = (16, 256)
        DT_MIN, DT_MAX = (0.001, 0.1)

        def _make_DPLR_HiPPO(N):
            P = np.sqrt(1 + 2 * np.arange(N))
            A = P[:, None] * P[None, :]
            A = np.tril(A) - np.diag(np.arange(N))
            nhippo = -A
            p = 0.5 * np.sqrt(2 * np.arange(1, N + 1) + 1.0)
            q = 2 * p
            S = nhippo + p[:, None] * q[None, :]
            Lambda, V = np.linalg.eig(S)
            Vc = V.conj().T
            p_t = Vc @ p
            q_t = Vc @ q.conj()
            return (Lambda, p_t, q_t, Vc)

        def _ri(z):
            return np.stack([z.real, z.imag], axis=-1).astype(np.float32)

        def _cplx(x_ri):
            return x_ri[..., 0] + 1j * x_ri[..., 1]

        def _s4_kernel(Lambda, p, q, B, Ct, step, L):
            Omega = jnp.exp(-2j * jnp.pi * (jnp.arange(L) / L))
            g = 2.0 / step * ((1.0 - Omega) / (1.0 + Omega))
            c = 2.0 / (1.0 + Omega)
            denom = g[:, None] - Lambda[None, :]
            cauchy = lambda v: (v[None, :] / denom).sum(-1)
            k00 = cauchy(Ct.conj() * B)
            k01 = cauchy(Ct.conj() * p)
            k10 = cauchy(q.conj() * B)
            k11 = cauchy(q.conj() * p)
            at_roots = c * (k00 - k01 * (1.0 / (1.0 + k11)) * k10)
            return jnp.fft.ifft(at_roots, L).real
        L = u.shape[-1]
        Lambda = _cplx(Lambda_ri)
        p = _cplx(p_ri)
        q = _cplx(q_ri)
        Vc = _cplx(Vc_ri)
        Ct = _cplx(Ct_ri).reshape(-1)
        B = (Vc @ Bp.astype(Vc.dtype)).reshape(-1)
        step = jnp.exp(log_step)[0]
        K = _s4_kernel(Lambda, p, q, B, Ct, step, L).astype(u.dtype)
        n = 2 * L
        y = jnp.fft.irfft(jnp.fft.rfft(u, n=n) * jnp.fft.rfft(K, n=n), n=n)[..., :L]
        return y + D[0] * u

    def _L0_ffn_ref(x, W, bias, A, Bf, coeffs, scales):
        import jax, jax.numpy as jnp
        import numpy as np
        out = jnp.einsum('bsd,od->bso', x, W) + bias
        xa = jnp.einsum('bsd,erd->ebsr', x, A)
        w = coeffs * scales
        upd = jnp.einsum('ebsr,eor,e->bso', xa, Bf, w)
        return out + upd
    x = L0_attn_u
    mod = (_silu(L0_c) @ L0_wmod).reshape(L0_c.shape[0], 6, 1, -1)
    sa, ca, ga, sb, cb, gb = (mod[:, 0], mod[:, 1], mod[:, 2], mod[:, 3], mod[:, 4], mod[:, 5])
    ga = (2 * (ga >= 0) - 1) * jnp.maximum(jnp.abs(ga), 0.25)
    gb = (2 * (gb >= 0) - 1) * jnp.maximum(jnp.abs(gb), 0.25)
    h = _layernorm(x, axis=-1) * (1 + ca) + sa
    x = x + ga * _L0_attn_ref(h, L0_attn_Lambda_ri, L0_attn_p_ri, L0_attn_q_ri, L0_attn_Vc_ri, L0_attn_Ct_ri, L0_attn_Bp, L0_attn_D, L0_attn_log_step)
    h = _layernorm(x, axis=-1) * (1 + cb) + sb
    x = x + gb * _L0_ffn_ref(h, L0_ffn_W, L0_ffn_bias, L0_ffn_A, L0_ffn_Bf, L0_ffn_coeffs, L0_ffn_scales)
    return x

_drawn_inputs = setup_inputs


def setup_inputs(seed=0):
    import zlib

    import numpy as np

    out = dict(_drawn_inputs(seed))
    spreads = {'L0_ffn_scales': (0.5, 0.6)}
    factors = {'L0_attn_Lambda_ri': 8.0,
     'L0_attn_p_ri': 8.0,
     'L0_attn_q_ri': 8.0,
     'L0_attn_Vc_ri': 8.0,
     'L0_attn_Ct_ri': 8.0,
     'L0_attn_Bp': 8.0,
     'L0_ffn_bias': 8.0,
     'L0_ffn_coeffs': 6.579}
    for name, (base, spread) in spreads.items():
        noise = np.random.default_rng([zlib.crc32(name.encode()), seed]).standard_normal(out[name].shape)
        drawn = base * np.exp(spread * noise) if base else spread * noise
        out[name] = jnp.asarray(drawn.astype(out[name].dtype))
    for name, factor in factors.items():
        out[name] = (out[name] * factor).astype(out[name].dtype)
    return out
```

```python
import math
from contextlib import ExitStack

import numpy as np

import concourse.bass as bass
from concourse import mybir

F32 = mybir.dt.float32
F32R = mybir.dt.float32r
ALU = mybir.AluOpType
ACT = mybir.ActivationFunctionType
AX = mybir.AxisListType

P = 128
D = 2048
ROWS = 4096
BATCH = 4
NB = D // P
G = 512
NG = ROWS // G
GPB = NG // BATCH
N_STATE = 64
NMOD = 6
SA, CA, GA, SB, CB, GB, GBIAS = range(NMOD + 1)
EPS = 1e-5
LN2 = math.log(2.0)
LN2_HI = 355.0 / 512.0
ROUND = 1.5 * 2.0 ** 23

MC = 1536
NR = NMOD * D // MC
MQ = MC // 4
W_RING = 4

CONV_BANKS = 6
BANKS = 8
NE = 16 * 16
ER = NE // P
HALF = D // 2
HB = HALF // P


def semaphores(nc, ctx, names):
    return {n: ctx.enter_context(nc.semaphore(n)) for n in names.split()}


def scalar_of(t, b, c):
    if isinstance(b, int):
        return t[:, b, c:c + 1]
    return t[:, bass.ds(b, 1), c:c + 1].rearrange("p b c -> p (b c)")


def entry_of(t, b, n):
    if isinstance(b, int):
        return t[:, b, 0:n]
    return t[:, bass.ds(b, 1), 0:n].rearrange("p b c -> p (b c)")


def of_group(t, g, b0, n):
    return t[bass.ds(g, 1), :, b0:b0 + n, :].rearrange("g p b r -> (g p) b r")


def over_groups(eng, step):
    step((0, 0, 0))
    with eng.Fori(0, (NG - 2) // 2) as i:
        step((2 * i + 1, 1, i))
        step((2 * i + 2, 0, i + 1))
    step((NG - 1, 1, BATCH - 1))


def following(group):
    g, par, b = group
    if isinstance(g, int):
        return (g + 1, 1 - par, (g + 1) // GPB)
    return (g + 1, 1 - par, b + 1 if par == 1 else b)


def is_first(group):
    return isinstance(group[0], int) and group[0] == 0


def is_last(group):
    return isinstance(group[0], int) and group[0] == NG - 1




def phase_k(nc, io, keep):
    with ExitStack() as ctx:
        sb = lambda n, s, d=F32: ctx.enter_context(nc.sbuf_tensor(n, s, d))
        st = sb("k_state", [P, 8])
        vc = sb("k_vc", [N_STATE, 2, P])
        bp = sb("k_bp", [N_STATE, 1])
        trig = sb("k_trig", [P, 2, D])
        cospj = sb("k_cospj", [P, NB])
        idft = sb("k_idft", [P, 2, P])
        unroll = sb("k_unroll", [P, NB, 2 * NB])
        ident = sb("k_ident", [P, P])
        flip = sb("k_flip", [P, P])
        scal = sb("k_scal", [P, 8])
        ex = sb("k_ex", [P, 4])
        exi = sb("k_exi", [P, 1], mybir.dt.int32)
        bvec = sb("k_b", [P, 2])
        V = sb("k_V", [P, 8])
        pr = sb("k_pr", [P, 2, 4, 4])
        vv = sb("k_vv", [P, 4, 2])
        den = sb("k_den", [P, D])
        tmp = sb("k_tmp", [P, D])
        sq = sb("k_sq", [P, D])
        sq2 = sb("k_sq2", [P, D])
        R = sb("k_R", [P, D])
        S8 = sb("k_S8", [P, NB, 8])
        w = sb("k_w", [P, 24, NB])
        Z1 = sb("k_Z1", [P, NB, 2])
        Z2 = sb("k_Z2", [P, NB, 2])
        Fs = sb("k_F", [P, 2 * NB])
        prod = sb("k_prod", [P, NB, 2 * NB])
        K = sb("k_K", [P, NB])
        KT = sb("k_KT", [NB, P])
        zero = sb("k_zero", [1, P])
        dsb = sb("k_D", [1, 1])
        strip = sb("k_strip", [P, D])
        ps = ctx.enter_context(nc.psum_tensor("k_ps", [P, 4, 512], F32))
        s = semaphores(nc, ctx, "k_in k_b_ps k_b_sb k_chain k_sq_rdy k_sq2_rdy k_den k_R_rdy k_V_rdy "
                          "k_S_ps k_Z k_F_ps k_K_rdy k_KT_ps k_KT_sb k_out k_strip_in k_strip_ps k_hi k_zero_rdy")
        block = ctx.enter_context(nc.Block())
        N_IN = 13

        @block.sync
        def _(sp):
            for dst, src in ((st[:], io["state"]), (vc[:], io["vcT"]), (bp[:], io["bp"]),
                             (cospj[:], io["cos_pj"]), (idft[:], io["idft"]), (ident[:], io["ident"]),
                             (dsb[:], io["dskip"]), (flip[:], io["flip"]), (keep["ones"][:], io["ones"]), (keep["eps"][:], io["eps"]), (scal[:, 0:1], io["log_step"].to_broadcast([P, 1])),
                             (trig[:], io["trig"].partition_broadcast(P)), (unroll[:], io["unroll"])):
                sp.dma_start(dst, src).then_inc(s["k_in"], 16)
            sp.wait_ge(s["k_zero_rdy"], 1)
            sp.dma_start(io["kpad"][0:P].rearrange("(a b) -> a b", a=1), zero[:]).then_inc(s["k_out"], 16)
            sp.wait_ge(s["k_KT_sb"], 1)
            sp.dma_start(io["kpad"][P:P + D].rearrange("(a b) -> a b", a=NB), KT[:]).then_inc(s["k_out"], 16)
            sp.wait_ge(s["k_out"], 32)
            src = io["kpad"][1:P + D]
            toeplitz = bass.AP(tensor=src.tensor, offset=src.offset, ap=[[1, P], [1, D]])
            sp.dma_start(strip[:], toeplitz).then_inc(s["k_strip_in"], 16)

        @block.scalar
        def _(act):
            act.wait_ge(s["k_in"], 16 * N_IN)
            nc.scalar.activation(sq[:], trig[:, 0, :], ACT.Square, scale=st[:, 0:1]).then_inc(s["k_sq_rdy"], 1)
            act.wait_ge(s["k_den"], 1)
            nc.scalar.activation(sq2[:], den[:], ACT.Square).then_inc(s["k_sq2_rdy"], 1)
            act.wait_ge(s["k_strip_ps"], 1)
            nc.scalar.activation(keep["S_hi"][:], ps[:].rearrange("p b r -> p (b r)"), ACT.Copy).then_inc(s["k_hi"], 1)

        @block.tensor
        def _(pe):
            pe.wait_ge(s["k_in"], 16 * N_IN)
            nc.tensor.matmul(ps[:, 0, 0:1], vc[:, 0, :], bp[:, 0:1], start=True, stop=True)
            nc.tensor.matmul(ps[:, 1, 0:1], vc[:, 1, :], bp[:, 0:1], start=True, stop=True).then_inc(s["k_b_ps"], 1)
            pe.wait_ge(s["k_R_rdy"], 1)
            pe.wait_ge(s["k_V_rdy"], 1)
            for j in range(NB):
                mm = nc.tensor.matmul(ps[:, 2, 8 * j:8 * j + 8], R[:, j:D:NB], V[:, :], start=True, stop=True)
            mm.then_inc(s["k_S_ps"], 1)
            pe.wait_ge(s["k_Z"], 1)
            nc.tensor.matmul(ps[:, 3, 0:2 * NB], idft[:, 0, :], Z1[:].rearrange("p j r -> p (j r)"),
                             start=True, stop=False)
            nc.tensor.matmul(ps[:, 3, 0:2 * NB], idft[:, 1, :], Z2[:].rearrange("p j r -> p (j r)"),
                             start=False, stop=True).then_inc(s["k_F_ps"], 1)
            pe.wait_ge(s["k_K_rdy"], 1)
            nc.tensor.transpose(ps[0:NB, 0, 0:P], K[:], ident[:]).then_inc(s["k_KT_ps"], 1)
            pe.wait_ge(s["k_strip_in"], 16)
            for n in range(4):
                mm = nc.tensor.matmul(ps[:, n, :], flip[:], strip[:, n * 512:(n + 1) * 512], start=True, stop=True)
            mm.then_inc(s["k_strip_ps"], 1)

        @block.vector
        def _(dve):
            done = [0]

            def link(ins):
                done[0] += 1
                ins.then_inc(s["k_chain"], 1)
                dve.wait_ge(s["k_chain"], done[0])

            v = nc.vector
            v.memset(zero[:], 0.0).then_inc(s["k_zero_rdy"], 1)
            dve.wait_ge(s["k_in"], 16 * N_IN)
            e = lambda n: ex[:, n:n + 1]
            link(v.tensor_scalar(e(0), scal[:, 0:1], -1.0, None, ALU.mult))
            link(v.tensor_scalar(e(1), e(0), 1.0 / LN2, ROUND, ALU.mult, ALU.add))
            link(v.tensor_scalar(e(1), e(1), -ROUND, None, ALU.add))
            link(v.scalar_tensor_tensor(e(2), e(1), -LN2_HI, e(0), ALU.mult, ALU.add))
            link(v.scalar_tensor_tensor(e(2), e(1), -(LN2 - LN2_HI), e(2), ALU.mult, ALU.add))
            link(v.tensor_scalar(e(3), e(2), 1.0 / math.factorial(8), 1.0 / math.factorial(7), ALU.mult, ALU.add))
            for n in range(6, -1, -1):
                link(v.tensor_scalar(e(3), e(3), e(2), 1.0 / math.factorial(n), ALU.mult, ALU.add))
            link(v.tensor_scalar(e(1), e(1), 127.0, -126.0, ALU.min, ALU.max))
            link(v.tensor_scalar(e(1), e(1), 127.0, 2.0 ** 23, ALU.add, ALU.mult))
            link(v.tensor_copy(exi[:], e(1)))
            link(v.tensor_tensor(scal[:, 1:2], e(3), exi[:].bitcast(F32), ALU.mult))
            v.tensor_scalar(scal[:, 2:3], scal[:, 1:2], 2.0, None, ALU.mult)
            v.tensor_scalar(scal[:, 3:4], st[:, 1:2], -1.0, None, ALU.mult)
            v.tensor_scalar(scal[0:64, 4:5], st[0:64, 0:1], -1.0, None, ALU.mult)
            v.tensor_copy(scal[64:128, 4:5], st[64:128, 1:2])
            v.memset(scal[0:64, 5:6], 0.0)
            link(v.tensor_scalar(scal[64:128, 5:6], scal[64:128, 1:2], -2.0, None, ALU.mult))
            link(v.tensor_scalar(tmp[:], trig[:, 1, :], scal[:, 2:3], None, ALU.mult))
            v.scalar_tensor_tensor(den[:], trig[:, 0, :], scal[:, 3:4], tmp[:], ALU.mult,
                                   ALU.add).then_inc(s["k_den"], 1)
            dve.wait_ge(s["k_b_ps"], 1)
            v.tensor_copy(bvec[:, 0:1], ps[:, 0, 0:1])
            link(v.tensor_copy(bvec[:, 1:2], ps[:, 1, 0:1]))
            U = {"C": (st[:, 6:7], st[:, 7:8]), "q": (st[:, 4:5], st[:, 5:6])}
            Wv = {"B": (bvec[:, 0:1], bvec[:, 1:2]), "p": (st[:, 2:3], st[:, 3:4])}
            pairs = [("C", "B"), ("C", "p"), ("q", "B"), ("q", "p")]
            for n, (a, b) in enumerate(pairs):
                (ur, ui), (wr, wi) = U[a], Wv[b]
                v.tensor_tensor(pr[:, 0, n, 0:1], ur, wr, ALU.mult)
                v.tensor_tensor(pr[:, 0, n, 1:2], ui, wi, ALU.mult)
                v.tensor_tensor(pr[:, 0, n, 2:3], ur, wi, ALU.mult)
                last = v.tensor_tensor(pr[:, 0, n, 3:4], ui, wr, ALU.mult)
            link(last)
            v.tensor_tensor(vv[:, :, 0], pr[:, 0, :, 0], pr[:, 0, :, 1], ALU.add)
            link(v.tensor_tensor(vv[:, :, 1], pr[:, 0, :, 2], pr[:, 0, :, 3], ALU.subtract))
            v.tensor_copy(V[0:64, :], vv[0:64, :, :].rearrange("p n r -> p (n r)"))
            Vh = V[64:128, :].rearrange("p (n r) -> p n r", r=2)
            v.tensor_scalar(Vh[:, :, 0], vv[64:128, :, 1], -1.0, None, ALU.mult)
            v.tensor_copy(Vh[:, :, 1], vv[64:128, :, 0]).then_inc(s["k_V_rdy"], 1)
            dve.wait_ge(s["k_sq_rdy"], 1)
            dve.wait_ge(s["k_sq2_rdy"], 1)
            link(v.tensor_tensor(sq[:], sq[:], sq2[:], ALU.add))
            v.reciprocal(sq2[:], sq[:])
            link(v.tensor_scalar(tmp[:], trig[:, 1, :], scal[:, 5:6], None, ALU.mult))
            link(v.scalar_tensor_tensor(den[:], trig[:, 0, :], scal[:, 4:5], tmp[:], ALU.mult, ALU.add))
            v.tensor_tensor(R[:], den[:], sq2[:], ALU.mult).then_inc(s["k_R_rdy"], 1)
            dve.wait_ge(s["k_S_ps"], 1)
            link(v.tensor_copy(S8[:].rearrange("p j n -> p (j n)"), ps[:, 2, 0:P]))
            r = lambda n: S8[:, :, 2 * n]
            i = lambda n: S8[:, :, 2 * n + 1]
            T = lambda n: w[:, n, :]
            mul, add, sub = ALU.mult, ALU.add, ALU.subtract
            v.tensor_tensor(T(0), cospj[:], r(3), mul)
            v.tensor_tensor(T(1), cospj[:], i(3), mul)
            v.tensor_tensor(T(2), r(1), r(2), mul)
            v.tensor_tensor(T(3), i(1), i(2), mul)
            v.tensor_tensor(T(4), r(1), i(2), mul)
            link(v.tensor_tensor(T(5), i(1), r(2), mul))
            v.tensor_scalar(T(6), T(0), 1.0, None, add)
            v.tensor_tensor(T(7), T(2), T(3), sub)
            link(v.tensor_tensor(T(8), T(4), T(5), add))
            v.tensor_tensor(T(9), T(6), T(6), mul)
            v.tensor_tensor(T(10), T(1), T(1), mul)
            v.tensor_tensor(T(11), T(7), T(6), mul)
            v.tensor_tensor(T(12), T(8), T(1), mul)
            v.tensor_tensor(T(13), T(8), T(6), mul)
            link(v.tensor_tensor(T(14), T(7), T(1), mul))
            v.tensor_tensor(T(15), T(9), T(10), add)
            v.tensor_tensor(T(16), T(11), T(12), add)
            link(v.tensor_tensor(T(17), T(13), T(14), sub))
            link(v.reciprocal(T(18), T(15)))
            link(v.tensor_tensor(T(19), T(18), cospj[:], mul))
            v.tensor_tensor(T(20), T(16), T(19), mul)
            link(v.tensor_tensor(T(21), T(17), T(19), mul))
            v.tensor_tensor(Z1[:, :, 0], r(0), T(20), sub)
            link(v.tensor_tensor(Z1[:, :, 1], i(0), T(21), sub))
            v.tensor_scalar(Z2[:, :, 0], Z1[:, :, 1], -1.0, None, mul)
            v.tensor_copy(Z2[:, :, 1], Z1[:, :, 0]).then_inc(s["k_Z"], 1)
            dve.wait_ge(s["k_F_ps"], 1)
            link(v.tensor_copy(Fs[:], ps[:, 3, 0:2 * NB]))
            link(v.tensor_tensor(prod[:], unroll[:], Fs[:].unsqueeze(1).broadcast_to([P, NB, 2 * NB]), mul))
            link(v.tensor_reduce(K[:], prod[:], AX.X, add))
            v.tensor_tensor(K[0:1, 0:1], K[0:1, 0:1], dsb[:], add).then_inc(s["k_K_rdy"], 1)
            dve.wait_ge(s["k_KT_ps"], 1)
            v.tensor_copy(KT[:], ps[0:NB, 0, 0:P]).then_inc(s["k_KT_sb"], 1)
            dve.wait_ge(s["k_hi"], 1)
            v.tensor_tensor(keep["S_lo"][:], ps[:].rearrange("p b r -> p (b r)"), keep["S_hi"][:], sub)




def phase_m(nc, io, keep):
    modT = keep["modT"]
    with ExitStack() as ctx:
        sb = lambda n, s, d=F32: ctx.enter_context(nc.sbuf_tensor(n, s, d))
        ct = sb("m_c", [P, NB, BATCH])
        ex = sb("m_ex", [P, NB, BATCH])
        rc = sb("m_rc", [P, NB, BATCH])
        sl = sb("m_silu", [P, NB, BATCH])
        ident = sb("m_ident", [P, P])
        bias = sb("m_bias", [P, NB])
        wt = sb("m_w", [P, W_RING, MC])
        rows = sb("m_rows", [P, 2, MQ])
        g1 = sb("m_g1", [P, BATCH, 2, NB])
        g2 = sb("m_g2", [P, BATCH, 2, NB])
        acc = ctx.enter_context(nc.psum_tensor("m_acc", [P, 2, 512], F32))
        tps = ctx.enter_context(nc.psum_tensor("m_tps", [P, 2, 512], F32))
        s = semaphores(nc, ctx, "m_in m_exp m_chain m_silu_rdy m_w_used m_acc_rdy m_rows_zero m_rows_rdy "
                          "m_tps_rdy m_mod_rdy")
        w_in = [ctx.enter_context(nc.semaphore(f"m_w_in{n}")) for n in range(W_RING)]
        block = ctx.enter_context(nc.Block())

        @block.sync
        def _(sp):
            for dst, src in ((ct[:], io["cT"]), (ident[:], io["ident"]), (bias[:], io["biasT"])):
                sp.dma_start(dst, src).then_inc(s["m_in"], 16)
            for n in range(NR * NB):
                r, k = divmod(n, NB)
                if n >= W_RING:
                    sp.wait_ge(s["m_w_used"], n - W_RING + 1)
                sp.dma_start(wt[:, n % W_RING, :], io["wmod"][k * P:(k + 1) * P, r * MC:(r + 1) * MC]
                             ).then_inc(w_in[n % W_RING], 16)

        @block.scalar
        def _(act):
            act.wait_ge(s["m_in"], 48)
            nc.scalar.activation(ex[:], ct[:], ACT.Exp, scale=-1.0).then_inc(s["m_exp"], 1)

        @block.tensor
        def _(pe):
            def transposes(r):
                pe.wait_ge(s["m_rows_rdy"], r + 1)
                if r >= 2:
                    pe.wait_ge(s["m_mod_rdy"], r - 1)
                for n in range(3):
                    mm = nc.tensor.transpose(tps[:, r % 2, n * P:(n + 1) * P], rows[:, r % 2, n * P:(n + 1) * P],
                                             ident[:])
                mm.then_inc(s["m_tps_rdy"], 1)

            pe.wait_ge(s["m_silu_rdy"], 1)
            for r in range(NR):
                if r >= 2:
                    pe.wait_ge(s["m_rows_rdy"], r - 1)
                for k in range(NB):
                    n = r * NB + k
                    pe.wait_ge(w_in[n % W_RING], 16 * (n // W_RING + 1))
                    for g in range(4):
                        mm = nc.tensor.matmul(acc[32 * g:32 * g + BATCH, r % 2, 0:MQ], sl[:, k, :],
                                              wt[:, n % W_RING, g * MQ:(g + 1) * MQ],
                                              start=(k == 0), stop=(k == NB - 1),
                                              tile_position=(0, 32 * g))
                    mm.then_inc(s["m_w_used"], 1)
                if r >= 1:
                    transposes(r - 1)
            transposes(NR - 1)

        @block.vector
        def _(dve):
            v = nc.vector
            done = [0]

            def link(ins):
                done[0] += 1
                ins.then_inc(s["m_chain"], 1)
                dve.wait_ge(s["m_chain"], done[0])

            def spread(r):
                dve.wait_ge(s["m_tps_rdy"], r + 1)
                src = tps[:, r % 2, 0:3 * P].rearrange("p (n g c) -> p n g c", n=3, g=4)
                for n in range(3):
                    dst = modT[:, :, 12 * r + n:12 * r + 12:3]
                    last = nc.vector.tensor_copy(dst, src[:, n, :, 0:BATCH].rearrange("p g b -> p b g"))
                last.then_inc(s["m_mod_rdy"], 1)

            link(v.memset(rows[:], 0.0))
            dve.wait_ge(s["m_exp"], 1)
            link(v.tensor_scalar(ex[:], ex[:], 1.0, None, ALU.add))
            link(v.reciprocal(rc[:], ex[:]))
            v.tensor_tensor(sl[:], ct[:], rc[:], ALU.mult).then_inc(s["m_silu_rdy"], 1)
            for r in range(NR):
                dve.wait_ge(s["m_w_used"], NB * (r + 1))
                if r >= 2:
                    dve.wait_ge(s["m_tps_rdy"], r - 1)
                for g in range(4):
                    last = v.tensor_copy(rows[32 * g:32 * g + BATCH, r % 2, :],
                                         acc[32 * g:32 * g + BATCH, r % 2, 0:MQ])
                last.then_inc(s["m_rows_rdy"], 1)
                if r >= 1:
                    spread(r - 1)
            spread(NR - 1)
            dve.wait_ge(s["m_mod_rdy"], NR)
            comp = lambda m, n=1: modT[:, :, m * NB:(m + n) * NB]
            v.tensor_scalar(comp(CA), comp(CA), 1.0, None, ALU.add)
            v.tensor_scalar(comp(CB), comp(CB), 1.0, None, ALU.add)
            for n, m in enumerate((GA, GB)):
                v.tensor_scalar(g1[:, :, n, :], comp(m), 0.0, 2.0, ALU.is_ge, ALU.mult)
                last = v.tensor_scalar(g2[:, :, n, :], comp(m), -1.0, None, ALU.mult)
            link(last)
            for n, m in enumerate((GA, GB)):
                last = v.tensor_tensor(g2[:, :, n, :], g2[:, :, n, :], comp(m), ALU.max)
            link(last)
            v.tensor_scalar(g1[:], g1[:], -1.0, None, ALU.add)
            link(v.tensor_scalar(g2[:], g2[:], 0.25, None, ALU.max))
            for n, m in enumerate((GA, GB)):
                last = v.tensor_tensor(comp(m), g1[:, :, n, :], g2[:, :, n, :], ALU.mult)
            link(last)
            for b in range(BATCH):
                v.tensor_tensor(modT[:, b, GBIAS * NB:], modT[:, b, GB * NB:(GB + 1) * NB], bias[:], ALU.mult)



AT_MEAN2, AT_VAR2, AT_MEAN1, AT_VAR1 = 4, 9, 11, 13


def phase_a(nc, io, keep):
    modT, S_hi, S_lo, ones, epsc = keep["modT"], keep["S_hi"], keep["S_lo"], keep["ones"], keep["eps"]
    with ExitStack() as ctx:
        sb = lambda n, s, d=F32: ctx.enter_context(nc.sbuf_tensor(n, s, d))
        X = [sb(f"a_x{n}", [P, NB, G]) for n in range(2)]
        H = sb("a_h", [P, NB, G])
        h_hi = sb("a_h_hi", [P, NB, G], F32R)
        h_lo = sb("a_h_lo", [P, NB, G], F32R)
        acc1 = sb("a_acc1", [P, G])
        acc2 = sb("a_acc2", [P, G])
        sqa = sb("a_sqa", [P, G])
        sq = sb("a_sq", [P, 2, 2, G])
        rstd = sb("a_rstd", [P, G])
        now = sb("a_now", [P, 2, NB])
        stat = sb("a_stat", [P, 2, G])
        conv = ctx.enter_context(nc.psum_tensor("a_conv", [P, CONV_BANKS, G], F32))
        mean = ctx.enter_context(nc.psum_tensor("a_mean", [P, G], F32))
        var = ctx.enter_context(nc.psum_tensor("a_var", [P, G], F32))
        s = semaphores(nc, ctx, "a_x_in0 a_x_in1 a_x2_out a_stat_out "
                          "a_hi_rdy a_lo_rdy a_hl_free a_conv_rdy a_x2_rdy "
                          "a_sum1 a_sum2 a_mean1 a_var1 a_mean2 a_var2 "
                          "a_now_rdy a_dev1 a_sq1_rdy a_sqa1 a_sd1 a_rstd1 a_u1 a_h_rdy "
                          "a_dev2 a_sq2_rdy a_sqa2 a_sd2 a_stat_rdy")
        block = ctx.enter_context(nc.Block())
        x_in = [s["a_x_in0"], s["a_x_in1"]]
        NC = 4
        CB4 = NB // NC

        @block.sync
        def _(sp):
            def load(group, c):
                g, par, _ = group
                sp.dma_start(X[par][:, c * CB4:(c + 1) * CB4, :],
                             of_group(io["x"], g, c * CB4, CB4)).then_inc(x_in[par], 16)

            def store(group, c):
                g, par, _ = group
                sp.wait_ge(s["a_x2_rdy"], NB * g + (c + 1) * CB4)
                sp.dma_start(of_group(io["x2"], g, c * CB4, CB4),
                             X[par][:, c * CB4:(c + 1) * CB4, :]).then_inc(s["a_x2_out"], 16)

            def store_stat(g):
                sp.wait_ge(s["a_stat_rdy"], g + 1)
                sp.dma_start(of_group(io["stat"], g, 0, 2), stat[:]).then_inc(s["a_stat_out"], 16)

            def step(group):
                g = group[0]
                store(group, 0)
                if not is_last(group):
                    for c in range(NC):
                        if is_first(group):
                            load(following(group), c)
                            continue
                        if c == 0:
                            sp.wait_ge(s["a_x2_out"], 16 * NC * g + 16)
                        sp.wait_ge(s["a_dev2"], (NB // 2) * (g - 1) + 2 * (c + 1))
                        load(following(group), c)
                store(group, 1)
                if not is_first(group):
                    store_stat(g - 1)
                store(group, 2)
                store(group, 3)

            for c in range(NC):
                load((0, 0, 0), c)
            over_groups(sp, step)
            store_stat(NG - 1)
            sp.wait_ge(s["a_x2_out"], 16 * NC * NG)
            sp.wait_ge(s["a_stat_out"], 16 * NG)

        @block.tensor
        def _(pe):
            mm = nc.tensor.matmul

            def total(out, acc, rdy, value, sem):
                pe.wait_ge(rdy, value)
                mm(out[:], ones[:], acc[:], start=True, stop=True).then_inc(sem, 1)

            def mean1(g):
                if not (isinstance(g, int) and g <= 1):
                    pe.wait_ge(s["a_stat_rdy"], g - 1)
                total(mean, acc1, s["a_sum1"], (NB - 1) * (g + 1), s["a_mean1"])

            def var1(g):
                total(var, sqa, s["a_sqa1"], (NB - 1) * (g + 1), s["a_var1"])

            def mean2(g):
                total(mean, acc2, s["a_sum2"], (NB - 1) * (g + 1), s["a_mean2"])

            def var2(g):
                total(var, sqa, s["a_sqa2"], (NB - 1) * (g + 1), s["a_var2"])

            def step(group):
                g = group[0]
                for j in range(NB):
                    if j == AT_MEAN2 and not is_first(group):
                        mean2(g - 1)
                    if j == AT_VAR2 and not is_first(group):
                        var2(g - 1)
                    if j == AT_MEAN1 and not is_last(group):
                        mean1(g + 1)
                    if j == AT_VAR1 and not is_last(group):
                        var1(g + 1)
                    pe.wait_ge(s["a_hi_rdy"], NB * g + j + 1)
                    pe.wait_ge(s["a_lo_rdy"], NB * g + j + 1)
                    conv_block(group, j)

            def conv_block(group, j):
                g, par, _ = group
                bank_free(g, j)
                out = conv[:, j % CONV_BANKS, :]
                for a in range(j + 1):
                    hi = S_hi[:, (j - a) * P:(j - a + 1) * P]
                    lo = S_lo[:, (j - a) * P:(j - a + 1) * P]
                    mm(out, hi, h_hi[:, a, :], start=(a == 0), stop=False)
                    mm(out, hi, h_lo[:, a, :], start=False, stop=False)
                    last = mm(out, lo, h_hi[:, a, :], start=False, stop=(a == j))
                    if j == NB - 1 and a < j:
                        last.then_inc(s["a_hl_free"], 1)
                last.then_inc(s["a_conv_rdy"], 1)

            def bank_free(g, j):
                if j >= CONV_BANKS:
                    pe.wait_ge(s["a_x2_rdy"], NB * g + j - CONV_BANKS + 1)
                elif not (isinstance(g, int) and g == 0):
                    prev = max(n for n in range(NB) if n % CONV_BANKS == j)
                    pe.wait_ge(s["a_x2_rdy"], NB * g - NB + prev + 1)

            mean1(0)
            var1(0)
            over_groups(pe, step)
            mean2(NG - 1)
            var2(NG - 1)

        @block.vector
        def _(dve):
            v = nc.vector
            NP2 = NB // 2

            def pair(t, n):
                return t[:, 2 * n:2 * n + 2, :]

            def twice(row):
                return row.unsqueeze(1).broadcast_to([P, 2, G])

            def epilogue(group, j):
                g, par, b = group
                dve.wait_ge(s["a_conv_rdy"], NB * g + j + 1)
                x = X[par][:, j, :]
                v.scalar_tensor_tensor(x, conv[:, j % CONV_BANKS, :], scalar_of(modT, b, GA * NB + j), x,
                                       ALU.mult, ALU.add).then_inc(s["a_x2_rdy"], 1)

            def add_squares(g, n, rdy, chain):
                dve.wait_ge(rdy, NP2 * g + n + 1)
                t = sq[:, n % 2]
                if n == 0:
                    v.tensor_tensor(sqa[:], t[:, 0, :], t[:, 1, :], ALU.add).then_inc(chain, 1)
                    return
                base = (NB - 1) * g + 2 * n - 1
                dve.wait_ge(chain, base)
                v.tensor_tensor(sqa[:], sqa[:], t[:, 0, :], ALU.add).then_inc(chain, 1)
                dve.wait_ge(chain, base + 1)
                v.tensor_tensor(sqa[:], sqa[:], t[:, 1, :], ALU.add).then_inc(chain, 1)

            def variance2(group, ns):
                g, par, _ = group
                for n in ns:
                    if n == 0:
                        dve.wait_ge(s["a_mean2"], g + 1)
                        last1 = min(g + 1, NG - 1) if isinstance(g, int) else g + 1
                        dve.wait_ge(s["a_sqa1"], (NB - 1) * (last1 + 1))
                        dve.wait_ge(s["a_u1"], NP2 * (last1 + 1))
                    if n >= 2:
                        dve.wait_ge(s["a_sqa2"], (NB - 1) * g + 2 * n - 3)
                    v.tensor_tensor(sq[:, n % 2], pair(X[par], n), twice(mean[:]), ALU.subtract
                                    ).then_inc(s["a_dev2"], 1)
                    if n > 0:
                        add_squares(g, n - 1, s["a_sq2_rdy"], s["a_sqa2"])
                    if n == NP2 - 1:
                        add_squares(g, n, s["a_sq2_rdy"], s["a_sqa2"])

            def variance1(group, ns):
                g, par, _ = group
                for n in ns:
                    if n == 0:
                        dve.wait_ge(s["a_mean1"], g + 1)
                        if not is_first(group):
                            dve.wait_ge(s["a_lo_rdy"], NB * g)
                    v.tensor_tensor(pair(H, n), pair(X[par], n), twice(mean[:]), ALU.subtract
                                    ).then_inc(s["a_dev1"], 1)
                    if n > 0:
                        add_squares(g, n - 1, s["a_sq1_rdy"], s["a_sqa1"])
                    if n == NP2 - 1:
                        add_squares(g, n, s["a_sq1_rdy"], s["a_sqa1"])

            def finish2(g):
                if not (isinstance(g, int) and g == 0):
                    dve.wait_ge(s["a_stat_out"], 16 * g)
                v.tensor_copy(stat[:, 0, :], mean[:])
                dve.wait_ge(s["a_sd2"], g + 1)
                v.reciprocal(stat[:, 1, :], rstd[:]).then_inc(s["a_stat_rdy"], 1)

            def scale1(group):
                g = group[0]
                dve.wait_ge(s["a_sd1"], g + 1)
                v.reciprocal(sqa[:], rstd[:]).then_inc(s["a_rstd1"], 1)
                dve.wait_ge(s["a_rstd1"], g + 1)
                for n in range(NP2):
                    v.tensor_tensor(pair(H, n), pair(H, n), twice(sqa[:]), ALU.mult).then_inc(s["a_u1"], 1)

            def step(group):
                g, par, b = group
                prev = (g - 1, 1 - par, None)
                nxt = following(group)
                first, last = is_first(group), is_last(group)
                E = lambda *js: [epilogue(group, j) for j in js]
                E(0, 1, 2, 3)
                if not first:
                    variance2(prev, range(0, 3))
                E(4)
                if not first:
                    variance2(prev, range(3, 6))
                E(5)
                if not first:
                    variance2(prev, range(6, 8))
                E(6, 7, 8)
                if not first:
                    finish2(g - 1)
                E(9, 10)
                if not last:
                    variance1(nxt, range(0, 4))
                E(11)
                if not last:
                    variance1(nxt, range(4, 8))
                E(12)
                if not last:
                    scale1(nxt)
                E(13, 14, 15)

            variance1((0, 0, 0), range(0, 8))
            scale1((0, 0, 0))
            over_groups(dve, step)
            variance2((NG - 1, 1, None), range(0, 8))
            finish2(NG - 1)

        @block.gpsimd
        def _(pool):
            v = nc.gpsimd

            def sum1(group, started):
                g, par, _ = group
                loads = g // 2 + 1 if isinstance(g, int) else None
                if not is_first(group):
                    pool.wait_ge(s["a_mean1"], g)
                for n in range(1, NB):
                    if n == 1:
                        pool.wait_ge(x_in[par], 16 * NC * loads if loads else 16 * NC * started)
                        v.tensor_tensor(acc1[:], X[par][:, 0, :], X[par][:, 1, :], ALU.add).then_inc(s["a_sum1"], 1)
                    else:
                        pool.wait_ge(s["a_sum1"], (NB - 1) * g + n - 1)
                        v.tensor_tensor(acc1[:], acc1[:], X[par][:, n, :], ALU.add).then_inc(s["a_sum1"], 1)

            def sum2(group, j):
                g, par, _ = group
                pool.wait_ge(s["a_x2_rdy"], NB * g + j + 1)
                if j == 0:
                    return
                if j == 1:
                    if not is_first(group):
                        pool.wait_ge(s["a_mean2"], g)
                    v.tensor_tensor(acc2[:], X[par][:, 0, :], X[par][:, 1, :], ALU.add).then_inc(s["a_sum2"], 1)
                    return
                pool.wait_ge(s["a_sum2"], (NB - 1) * g + j - 1)
                v.tensor_tensor(acc2[:], acc2[:], X[par][:, j, :], ALU.add).then_inc(s["a_sum2"], 1)

            def low(g, a):
                pool.wait_ge(s["a_hi_rdy"], NB * g + a + 1)
                v.tensor_tensor(h_lo[:, a, :], H[:, a, :], h_hi[:, a, :], ALU.subtract).then_inc(s["a_lo_rdy"], 1)

            def step(group):
                g, par, b = group
                for j in range(0, 9):
                    sum2(group, j)
                if not is_last(group):
                    started = None if isinstance(g, int) else (b + 2 if par == 1 else b + 1)
                    sum1(following(group), started)
                for j in range(9, NB - 1):
                    sum2(group, j)
                if not is_last(group):
                    for a in range(0, 8):
                        low(g + 1, a)
                sum2(group, NB - 1)
                if not is_last(group):
                    for a in range(8, NB):
                        low(g + 1, a)

            sum1((0, 0, 0), None)
            for a in range(NB):
                low(0, a)
            over_groups(pool, step)

        @block.scalar
        def _(act):
            NP2 = NB // 2

            def squares1(group):
                g = group[0]
                for n in range(NP2):
                    act.wait_ge(s["a_dev1"], NP2 * g + n + 1)
                    if n >= 2:
                        act.wait_ge(s["a_sqa1"], (2 * NP2 - 1) * g + 2 * (n - 2) + 1)
                    nc.scalar.activation(sq[:, n % 2], H[:, 2 * n:2 * n + 2, :], ACT.Square).then_inc(s["a_sq1_rdy"], 1)

            def squares2(g):
                for n in range(NP2):
                    act.wait_ge(s["a_dev2"], NP2 * g + n + 1)
                    nc.scalar.activation(sq[:, n % 2], sq[:, n % 2], ACT.Square).then_inc(s["a_sq2_rdy"], 1)

            def sigma(var_rdy, g, done):
                act.wait_ge(var_rdy, g + 1)
                nc.scalar.activation(rstd[:], var[:], ACT.Sqrt, bias=epsc[:, 0:1]).then_inc(done, 1)

            def modulate(group, a):
                if a % 2 == 0:
                    act.wait_ge(s["a_u1"], NP2 * group[0] + a // 2 + 1)
                nc.scalar.activation(H[:, a, :], H[:, a, :], ACT.Identity, scale=now[:, CA, a:a + 1],
                                     bias=now[:, SA, a:a + 1]).then_inc(s["a_h_rdy"], 1)

            def high(group, a):
                g = group[0]
                act.wait_ge(s["a_h_rdy"], NB * g + a + 1)
                if not (isinstance(g, int) and g == 0):
                    if a < NB - 1:
                        act.wait_ge(s["a_hl_free"], (NB - 1) * g - (NB - 1) + a + 1)
                    else:
                        act.wait_ge(s["a_conv_rdy"], NB * g)
                nc.scalar.activation(h_hi[:, a, :], H[:, a, :], ACT.Copy).then_inc(s["a_hi_rdy"], 1)

            def split(group):
                g, _, b = group
                nc.scalar.activation(now[:].rearrange("p m c -> p (m c)"), entry_of(modT, b, 2 * NB), ACT.Copy
                                     ).then_inc(s["a_now_rdy"], 1)
                act.wait_ge(s["a_now_rdy"], g + 1)
                for a in range(NB):
                    modulate(group, a)
                    if a:
                        high(group, a - 1)
                high(group, NB - 1)

            def step(group):
                g = group[0]
                if not is_first(group):
                    squares2(g - 1)
                    sigma(s["a_var2"], g - 1, s["a_sd2"])
                if not is_last(group):
                    squares1(following(group))
                    sigma(s["a_var1"], g + 1, s["a_sd1"])
                    split(following(group))

            squares1((0, 0, 0))
            sigma(s["a_var1"], 0, s["a_sd1"])
            split((0, 0, 0))
            over_groups(act, step)
            squares2(NG - 1)
            sigma(s["a_var2"], NG - 1, s["a_sd2"])




def phase_f(nc, io, keep, half):
    W_hi, W_lo = keep["W_hi"], keep["W_lo"]
    NT = NB * 2
    RING = 4
    with ExitStack() as ctx:
        nm = lambda n: f"f{half}_{n}"
        sb = lambda n, s, d=F32: ctx.enter_context(nc.sbuf_tensor(nm(n), s, d))
        wsc = sb("wsc", [P, 2, ER])
        ws = sb("ws", [P, ER])
        bf = sb("bf", [P, ER, HALF])
        bf_hi = sb("bf_hi", [P, ER, HALF], F32R)
        bf_lo = sb("bf_lo", [P, ER, HALF], F32R)
        A = sb("A", [P, NB, ER, P])
        A_hi = sb("A_hi", [P, 2, ER, P], F32R)
        A_lo = sb("A_lo", [P, 2, ER, P], F32R)
        W = sb("W", [P, RING, G])
        ps = ctx.enter_context(nc.psum_tensor(nm("ps"), [P, BANKS, G], F32))
        sems = {n: ctx.enter_context(nc.semaphore(nm(n))) for n in
                "in A_in ws_rdy bf_sc bf_hi_rdy bf_lo_rdy A_hi_rdy A_lo_rdy ps_rdy sum_rdy hi_rdy lo_rdy".split()}
        W_in = [ctx.enter_context(nc.semaphore(nm(f"W_in{n}"))) for n in range(RING)]
        block = ctx.enter_context(nc.Block())

        @block.sync
        def _(sp):
            sp.dma_start(wsc[:], io["wsc"]).then_inc(sems["in"], 16)
            sp.dma_start(bf[:], io["bf"][half]).then_inc(sems["in"], 16)
            sp.dma_start(A[:], io["A"]).then_inc(sems["A_in"], 16)
            for n in range(NT):
                d, c = divmod(n, 2)
                if n >= RING:
                    sp.wait_ge(sems["hi_rdy"], n - RING + 1)
                    sp.wait_ge(sems["lo_rdy"], n - RING + 1)
                sp.dma_start(W[:, n % RING, :], io["W"][half, d, :, c * G:(c + 1) * G]).then_inc(W_in[n % RING], 16)

        @block.tensor
        def _(pe):
            pe.wait_ge(sems["bf_hi_rdy"], 1)
            pe.wait_ge(sems["bf_lo_rdy"], 1)
            for n in range(NT):
                d, c = divmod(n, 2)
                if c == 0:
                    pe.wait_ge(sems["A_hi_rdy"], d + 1)
                    pe.wait_ge(sems["A_lo_rdy"], d + 1)
                if n >= BANKS:
                    pe.wait_ge(sems["sum_rdy"], n - BANKS + 1)
                out = ps[:, n % BANKS, :]
                for e in range(ER):
                    cols = slice(c * G, (c + 1) * G)
                    nc.tensor.matmul(out, A_hi[:, d % 2, e, :], bf_hi[:, e, cols], start=(e == 0), stop=False)
                    nc.tensor.matmul(out, A_hi[:, d % 2, e, :], bf_lo[:, e, cols], start=False, stop=False)
                    mm = nc.tensor.matmul(out, A_lo[:, d % 2, e, :], bf_hi[:, e, cols], start=False,
                                          stop=(e == ER - 1))
                mm.then_inc(sems["ps_rdy"], 1)

        @block.vector
        def _(dve):
            v = nc.vector
            dve.wait_ge(sems["in"], 32)
            v.tensor_tensor(ws[:], wsc[:, 0, :], wsc[:, 1, :], ALU.mult).then_inc(sems["ws_rdy"], 1)
            dve.wait_ge(sems["ws_rdy"], 1)
            for e in range(ER):
                v.tensor_scalar(bf[:, e, :], bf[:, e, :], ws[:, e:e + 1], None, ALU.mult).then_inc(sems["bf_sc"], 1)
            dve.wait_ge(sems["bf_hi_rdy"], 1)
            v.tensor_tensor(bf_lo[:], bf[:], bf_hi[:], ALU.subtract).then_inc(sems["bf_lo_rdy"], 1)

            def a_low(d):
                dve.wait_ge(sems["A_hi_rdy"], d + 1)
                v.tensor_tensor(A_lo[:, d % 2], A[:, d], A_hi[:, d % 2], ALU.subtract).then_inc(sems["A_lo_rdy"], 1)

            a_low(0)
            a_low(1)
            for n in range(NT):
                d, c = divmod(n, 2)
                dve.wait_ge(sems["ps_rdy"], n + 1)
                dve.wait_ge(W_in[n % RING], 16 * (n // RING + 1))
                v.tensor_tensor(W[:, n % RING, :], W[:, n % RING, :], ps[:, n % BANKS, :],
                                ALU.add).then_inc(sems["sum_rdy"], 1)
                if c == 1 and d + 2 < NB:
                    a_low(d + 2)

        @block.scalar
        def _(act):
            act.wait_ge(sems["bf_sc"], ER)
            nc.scalar.activation(bf_hi[:], bf[:], ACT.Copy).then_inc(sems["bf_hi_rdy"], 1)
            act.wait_ge(sems["A_in"], 16)

            def a_high(d):
                if d >= 2:
                    act.wait_ge(sems["ps_rdy"], 2 * (d - 1))
                nc.scalar.activation(A_hi[:, d % 2], A[:, d], ACT.Copy).then_inc(sems["A_hi_rdy"], 1)

            a_high(0)
            a_high(1)
            for n in range(NT):
                d, c = divmod(n, 2)
                if c == 0 and d >= 1 and d + 1 < NB:
                    a_high(d + 1)
                act.wait_ge(sems["sum_rdy"], n + 1)
                nc.scalar.activation(W_hi[:, d, c * G:(c + 1) * G], W[:, n % RING, :], ACT.Copy
                                     ).then_inc(sems["hi_rdy"], 1)

        @block.gpsimd
        def _(pool):
            for n in range(NT):
                d, c = divmod(n, 2)
                cols = slice(c * G, (c + 1) * G)
                pool.wait_ge(sems["hi_rdy"], n + 1)
                nc.gpsimd.tensor_tensor(W_lo[:, d, cols], W[:, n % RING, :], W_hi[:, d, cols],
                                        ALU.subtract).then_inc(sems["lo_rdy"], 1)




def phase_b(nc, io, keep, half):
    modT, W_hi, W_lo = keep["modT"], keep["W_hi"], keep["W_lo"]
    order = [(HB * (1 - half) + n) % NB for n in range(NB)]
    T_RING, HL_RING, O_RING = 4, 4, 4
    NH = NB // 2
    PART = 4
    AHEAD = 3
    with ExitStack() as ctx:
        nm = lambda n: f"b{half}_{n}"
        sb = lambda n, s, d=F32: ctx.enter_context(nc.sbuf_tensor(nm(n), s, d))
        X2 = sb("x2", [P, NB, G])
        T = sb("t", [P, T_RING, G])
        h_hi = sb("hi", [P, HL_RING, G], F32R)
        h_lo = sb("lo", [P, HL_RING, G], F32R)
        stat = sb("stat", [P, GPB, 2, G])
        O = sb("o", [P, O_RING, G])
        now = sb("now", [P, GPB, (NMOD + 1) * NB])
        ps = ctx.enter_context(nc.psum_tensor(nm("ps"), [P, BANKS, G], F32))
        S = {n: ctx.enter_context(nc.semaphore(nm(n))) for n in
             "now_rdy early_in late_in dev u h_rdy hi_rdy lo_rdy hl_free ps_rdy gated out_rdy".split()}
        stat_in = [ctx.enter_context(nc.semaphore(nm(f"stat_in{n}"))) for n in range(GPB)]
        stored = [ctx.enter_context(nc.semaphore(nm(f"stored{n}"))) for n in range(O_RING)]
        block = ctx.enter_context(nc.Block())

        @block.sync
        def _(sp):
            def load(group, k0, sem):
                for k in range(k0, k0 + NH, PART):
                    sp.dma_start(X2[:, k:k + PART, :], of_group(io["x2"], group[0], order[k], PART)
                                 ).then_inc(sem, 16)

            def load_early(group):
                g, par, _ = group
                sp.dma_start(stat[:, par], of_group(io["stat"], g, 0, 2)).then_inc(stat_in[par], 16)
                load(group, 0, S["early_in"])

            def step(group):
                g = group[0]
                if not is_last(group):
                    sp.wait_ge(S["dev"], NB * g + NH)
                    load_early(following(group))
                for o in range(HB):
                    sp.wait_ge(S["out_rdy"], HB * g + o + 1)
                    sp.dma_start(of_group(io["out"], g, half * HB + o, 1), O[:, o % O_RING:o % O_RING + 1, :]
                                 ).then_inc(stored[o % O_RING], 16)
                if not is_last(group):
                    load(following(group), NH, S["late_in"])

            load_early((0, 0, 0))
            load((0, 0, 0), NH, S["late_in"])
            over_groups(sp, step)
            for n in range(O_RING):
                sp.wait_ge(stored[n], 16 * NG * (HB // O_RING))

        @block.vector
        def _(dve):
            v = nc.vector

            def step(group):
                g, par, b = group
                loads = g // GPB + 1 if isinstance(g, int) else (b + 1)
                for k in range(NB):
                    n = NB * g + k
                    if k == 0:
                        dve.wait_ge(stat_in[par], 16 * loads)
                        dve.wait_ge(S["early_in"], 32 * (g + 1))
                    if k == NH:
                        dve.wait_ge(S["late_in"], 32 * (g + 1))
                    if not (is_first(group) and k < T_RING):
                        dve.wait_ge(S["lo_rdy"], n - T_RING + 1)
                    t = T[:, k % T_RING, :]
                    v.tensor_tensor(t, X2[:, k, :], stat[:, par, 0, :], ALU.subtract).then_inc(S["dev"], 1)
                    dve.wait_ge(S["dev"], n + 1)
                    v.tensor_tensor(t, t, stat[:, par, 1, :], ALU.mult).then_inc(S["u"], 1)

            over_groups(dve, step)

        @block.scalar
        def _(act):
            def modulate(group, k):
                g, par, b = group
                if k == 0:
                    nc.scalar.activation(now[:, par, :], entry_of(modT, b, (NMOD + 1) * NB), ACT.Copy
                                         ).then_inc(S["now_rdy"], 1)
                    act.wait_ge(S["now_rdy"], g + 1)
                act.wait_ge(S["u"], NB * g + k + 1)
                t = T[:, k % T_RING, :]
                nc.scalar.activation(t, t, ACT.Identity, scale=now[:, par, CB * NB + order[k]:CB * NB + order[k] + 1],
                                     bias=now[:, par, SB * NB + order[k]:SB * NB + order[k] + 1]
                                     ).then_inc(S["h_rdy"], 1)

            def high(group, k):
                g = group[0]
                act.wait_ge(S["h_rdy"], NB * g + k + 1)
                if k >= HL_RING:
                    act.wait_ge(S["hl_free"], (NB - 1) * g + k - HL_RING + 1)
                elif k < HL_RING - 1 and not is_first(group):
                    act.wait_ge(S["hl_free"], (NB - 1) * (g - 1) + NB + k - HL_RING + 1)
                elif not is_first(group):
                    act.wait_ge(S["ps_rdy"], HB * g)
                nc.scalar.activation(h_hi[:, k % HL_RING, :], T[:, k % T_RING, :], ACT.Copy).then_inc(S["hi_rdy"], 1)

            def split(group, ks):
                for k in ks:
                    modulate(group, k)
                    high(group, k)

            def gate(group, o):
                g, par, _ = group
                blk = half * HB + o
                act.wait_ge(S["ps_rdy"], HB * g + o + 1)
                if not (is_first(group) and o < O_RING):
                    act.wait_ge(stored[o % O_RING], 16 * ((HB // O_RING) * g + o // O_RING))
                nc.scalar.activation(O[:, o % O_RING, :], ps[:, o, :], ACT.Identity,
                                     scale=now[:, par, GB * NB + blk:GB * NB + blk + 1],
                                     bias=now[:, par, GBIAS * NB + blk:GBIAS * NB + blk + 1]
                                     ).then_inc(S["gated"], 1)

            def step(group):
                split(group, range(AHEAD, NB))
                if not is_last(group):
                    split(following(group), range(AHEAD))
                for o in range(HB):
                    gate(group, o)

            split((0, 0, 0), range(AHEAD))
            over_groups(act, step)

        @block.gpsimd
        def _(pool):
            def low(group, ks):
                for k in ks:
                    pool.wait_ge(S["hi_rdy"], NB * group[0] + k + 1)
                    nc.gpsimd.tensor_tensor(h_lo[:, k % HL_RING, :], T[:, k % T_RING, :], h_hi[:, k % HL_RING, :],
                                            ALU.subtract).then_inc(S["lo_rdy"], 1)

            def step(group):
                low(group, range(AHEAD, NB))
                if not is_last(group):
                    low(following(group), range(AHEAD))
                for o in range(HB):
                    pool.wait_ge(S["gated"], HB * group[0] + o + 1)
                    nc.gpsimd.tensor_tensor(O[:, o % O_RING, :], O[:, o % O_RING, :], X2[:, NH + o, :],
                                            ALU.add).then_inc(S["out_rdy"], 1)

            low((0, 0, 0), range(AHEAD))
            over_groups(pool, step)

        @block.tensor
        def _(pe):
            mm = nc.tensor.matmul

            def step(group):
                g = group[0]
                for k in range(NB):
                    pe.wait_ge(S["hi_rdy"], NB * g + k + 1)
                    pe.wait_ge(S["lo_rdy"], NB * g + k + 1)
                    hi, lo = h_hi[:, k % HL_RING, :], h_lo[:, k % HL_RING, :]
                    for o in range(HB):
                        if k == 0 and not is_first(group):
                            pe.wait_ge(S["gated"], HB * (g - 1) + o + 1)
                        cols = slice(o * P, (o + 1) * P)
                        w_hi, w_lo = W_hi[:, order[k], cols], W_lo[:, order[k], cols]
                        mm(ps[:, o, :], w_hi, hi, start=(k == 0), stop=False)
                        mm(ps[:, o, :], w_hi, lo, start=False, stop=False)
                        last = mm(ps[:, o, :], w_lo, hi, start=False, stop=(k == NB - 1))
                        if k == NB - 1:
                            last.then_inc(S["ps_rdy"], 1)
                    if k < NB - 1:
                        last.then_inc(S["hl_free"], 1)

            over_groups(pe, step)




def build(nc, io):
    with ExitStack() as top:
        sb = lambda ctx, n, s, d=F32: ctx.enter_context(nc.sbuf_tensor(n, s, d))
        keep = {
            "modT": sb(top, "modT", [P, BATCH, (NMOD + 1) * NB]),
            "ones": sb(top, "ones", [P, P]),
            "eps": sb(top, "eps", [P, 1]),
        }
        with ExitStack() as conv:
            keep["S_hi"] = sb(conv, "S_hi", [P, D], F32R)
            keep["S_lo"] = sb(conv, "S_lo", [P, D], F32R)
            phase_k(nc, io, keep)
            phase_m(nc, io, keep)
            phase_a(nc, io, keep)
        with ExitStack() as layer:
            keep["W_hi"] = sb(layer, "W_hi", [P, NB, HALF], F32R)
            keep["W_lo"] = sb(layer, "W_lo", [P, NB, HALF], F32R)
            for half in range(2):
                phase_f(nc, io, keep, half)
                phase_b(nc, io, keep, half)


def shape_tables():
    l = np.arange(D)
    theta = np.pi * l / D
    trig = np.stack([np.cos(theta), np.sin(theta)])
    trig[0, D // 2] = 0.0
    p, j, t1 = np.arange(P), np.arange(NB), np.arange(NB)
    t2 = np.arange(P)
    a = 2 * np.pi * np.outer(p, t2) / P + np.pi * p[:, None] / P
    u = (2 * np.pi * j[None, None, :] * t2[:, None, None] / D + np.pi * j[None, None, :] / D
         + 2 * np.pi * j[None, None, :] * t1[None, :, None] / NB)
    unroll = np.stack([np.cos(u), -np.sin(u)], axis=-1) / D
    return {
        "trig": trig,
        "cos_pj": trig[0].reshape(P, NB),
        "idft": np.stack([np.cos(a), np.sin(a)], axis=1),
        "unroll": unroll.reshape(P, NB, 2 * NB),
        "ident": np.eye(P),
        "flip": np.eye(P)[::-1],
        "ones": np.full((P, P), 1.0 / D),
        "eps": np.full((P, 1), EPS),
    }


def kernel(**inputs):
    import concourse.bacc as bacc
    from concourse.bass_utils import run_bass_kernel_spmd

    A = {k.removeprefix("L0_"): np.asarray(v) for k, v in inputs.items()}
    twice = lambda a: np.concatenate([a, a], axis=0)
    state = np.concatenate([A["attn_Lambda_ri"], A["attn_p_ri"], A["attn_q_ri"],
                            A["attn_Ct_ri"].reshape(N_STATE, 2)], axis=1)
    per_row = lambda a: np.repeat(a, NE // a.shape[0]).reshape(ER, P).T
    arrays = {
        "x": A["attn_u"].reshape(NG, G, NB, P).transpose(0, 3, 2, 1),
        "state": twice(state),
        "vcT": np.concatenate([A["attn_Vc_ri"].transpose(1, 2, 0)] * 2, axis=2),
        "bp": A["attn_Bp"],
        "dskip": A["attn_D"].reshape(1, 1),
        "log_step": A["attn_log_step"].reshape(1, 1),
        "cT": A["c"].T.reshape(NB, P, BATCH).transpose(1, 0, 2),
        "wmod": A["wmod"],
        "biasT": A["ffn_bias"].reshape(NB, P).T,
        "W": A["ffn_W"].T.reshape(NB, P, 2, HALF).transpose(2, 0, 1, 3),
        "A": A["ffn_A"].reshape(ER, P, NB, P).transpose(1, 2, 0, 3),
        "bf": A["ffn_Bf"].transpose(0, 2, 1).reshape(ER, P, 2, HALF).transpose(2, 1, 0, 3),
        "wsc": np.stack([per_row(A["ffn_coeffs"]), per_row(A["ffn_scales"])], axis=1),
    }
    arrays.update({n: t.astype(np.float32) for n, t in shape_tables().items()})
    arrays = {n: np.ascontiguousarray(a) for n, a in arrays.items()}

    nc = bacc.Bacc("TRN2", target_bir_lowering=False, num_devices=1)
    io = {n: nc.dram_tensor(f"in_{n}", a.shape, F32, kind="ExternalInput").ap() for n, a in arrays.items()}
    io["out"] = nc.dram_tensor("out", (NG, P, NB, G), F32, kind="ExternalOutput").ap()
    io["x2"] = nc.dram_tensor("x2_scratch", (NG, P, NB, G), F32).ap()
    io["stat"] = nc.dram_tensor("stat_scratch", (NG, P, 2, G), F32).ap()
    io["kpad"] = nc.dram_tensor("k_scratch", (P + D,), F32).ap()
    build(nc, io)
    r = run_bass_kernel_spmd(nc, [{f"in_{n}": a for n, a in arrays.items()}], core_ids=[0])
    out = r.results[0]["out"]
    return np.ascontiguousarray(out.transpose(0, 3, 2, 1)).reshape(BATCH, ROWS // BATCH, D)
```

```python
import math
from contextlib import ExitStack

import numpy as np

import concourse.bass as bass
from concourse import mybir

F32 = mybir.dt.float32
F32R = mybir.dt.float32r
ALU = mybir.AluOpType
ACT = mybir.ActivationFunctionType
AX = mybir.AxisListType

P = 128
D = 2048
ROWS = 4096
BATCH = 4
NB = D // P
G = 512
NG = ROWS // G
GPB = NG // BATCH
N_STATE = 64
NMOD = 6
SA, CA, GA, SB, CB, GB, GBIAS = range(NMOD + 1)
EPS = 1e-5
LN2 = math.log(2.0)
LN2_HI = 355.0 / 512.0
ROUND = 1.5 * 2.0 ** 23

CONV_BANKS = 5
BANKS = 8
NE = 16 * 16
ER = NE // P
HALF = D // 2
HB = HALF // P


def semaphores(nc, ctx, names):
    return {n: ctx.enter_context(nc.semaphore(n)) for n in names.split()}


def scalar_of(t, b, c):
    if isinstance(b, int):
        return t[:, b, c:c + 1]
    return t[:, bass.ds(b, 1), c:c + 1].rearrange("p b c -> p (b c)")


def entry_of(t, b, n):
    if isinstance(b, int):
        return t[:, b, 0:n]
    return t[:, bass.ds(b, 1), 0:n].rearrange("p b c -> p (b c)")


def of_group(t, g, b0, n):
    return t[bass.ds(g, 1), :, b0:b0 + n, :].rearrange("g p b r -> (g p) b r")


def over_groups(eng, step):
    step((0, 0, 0))
    over_later_groups(eng, step)


def over_later_groups(eng, step):
    with eng.Fori(0, (NG - 2) // 2) as i:
        step((2 * i + 1, 1, i))
        step((2 * i + 2, 0, i + 1))
    step((NG - 1, 1, BATCH - 1))


def following(group):
    g, par, b = group
    if isinstance(g, int):
        return (g + 1, 1 - par, (g + 1) // GPB)
    return (g + 1, 1 - par, b + 1 if par == 1 else b)


def is_first(group):
    return isinstance(group[0], int) and group[0] == 0


def is_last(group):
    return isinstance(group[0], int) and group[0] == NG - 1



UNITS = [(j, a) for j in range(NB) for a in range(j + 1)]
NU = len(UNITS)
AT_MEAN2, AT_VAR2, AT_MEAN1, AT_VAR1 = 14, 52, 66, 106
AT_TILE = [10 + 13 * k // 2 for k in range(NB)]
AT_TURN = 122
SLICES = 4
SLICE = NB // SLICES
SW = SLICE * P
NW1 = SLICES * NB
W1_RING = 4
W2_COLS = 3 * D // 6
W2_RING = 2
TURNS = W2_COLS // 4 // P
NC = 4
CB4 = NB // NC
KB = 1024
KH = D // 2


def phase_a(nc, io, keep):
    modT, S_hi, S_lo, ones, epsc = keep["modT"], keep["S_hi"], keep["S_lo"], keep["ones"], keep["eps"]
    with ExitStack() as ctx:
        sb = lambda n, s, d=F32: ctx.enter_context(nc.sbuf_tensor(n, s, d))
        base = nc.sbuf_base
        sb("a_slab", [P, 168 * KB // 4])
        at = lambda n, kib, s, d=F32: nc.alloc_sbuf_tensor_at(n, s, d, offset=base + int(kib * KB))
        X = [at(f"a_x{n}", 32 * n, [P, NB, G]) for n in range(2)]
        H = at("a_h", 64, [P, NB, G])
        h_hi = at("a_h_hi", 96, [P, NB, G], F32R)
        h_lo = at("a_h_lo", 128, [P, NB, G], F32R)
        w2 = at("a_w2", 160, [P, W2_RING, W2_COLS])
        w1 = [at(f"a_w1{n}", kib, [P, W1_RING, SW]) for n, kib in enumerate((120, 152, 160))]
        trig = at("k_trig", 32, [P, 2, KH])
        kt = [at(f"k_t{n}", 40 + 4 * n, [P, KH]) for n in range(6)]
        strip = at("k_strip", 40, [P, D])
        idft = at("k_idft", 128, [P, 2, P])
        unroll = at("k_unroll", 129, [P, NB, 2 * NB])
        prod = at("k_prod", 131, [P, NB, 2 * NB])
        vc = at("k_vc", 133, [N_STATE, 2, P])
        flip = at("k_flip", 134, [P, P])
        S8 = at("k_S8", 134.5, [P, NB, 8])
        w = at("k_w", 135, [P, 22, NB])
        KT = at("k_KT", 136.5, [NB, P])
        zero = at("k_zero", 137, [1, P])
        st = at("k_state", 138, [P, 8])
        bp = at("k_bp", 138.125, [N_STATE, 1])
        cospj = at("k_cospj", 138.25, [P, NB])
        scal = at("k_scal", 138.375, [P, 8])
        ex = at("k_ex", 138.5, [P, 4])
        exi = at("k_exi", 138.625, [P, 1], mybir.dt.int32)
        bvec = at("k_b", 138.75, [P, 2])
        V = at("k_V", 138.875, [P, 2, 8])
        pr = at("k_pr", 139, [P, 4, 4])
        vv = at("k_vv", 139.125, [P, 4, 2])
        Z1 = at("k_Z1", 139.25, [P, NB, 2])
        Z2 = at("k_Z2", 139.5, [P, NB, 2])
        Fs = at("k_F", 139.75, [P, 2 * NB])
        K = at("k_K", 140, [P, NB])
        dsb = at("k_D", 140.125, [1, 1])

        acc1 = sb("a_acc1", [P, G])
        acc2 = sb("a_acc2", [P, G])
        sqa = sb("a_sqa", [P, G])
        sq = sb("a_sq", [P, 2, 2, G])
        stat = sb("a_stat", [P, 2, G])
        now = sb("a_now", [P, 2, NB])
        ident = sb("m_ident", [P, P])
        rows = sb("m_rows", [P, SW])
        ct = sb("m_c", [P, NB, BATCH])
        ce = sb("m_ce", [P, NB, BATCH])
        sl = sb("m_silu", [P, NB, BATCH])
        bias = sb("m_bias", [P, NB])
        g1, g2 = (t[:].rearrange("p n b -> p (n b)").rearrange("p (b n) -> p b n", b=BATCH) for t in (ct, ce))
        conv = ctx.enter_context(nc.psum_tensor("a_conv", [P, CONV_BANKS, G], F32))
        mean = ctx.enter_context(nc.psum_tensor("a_mean", [P, G], F32))
        var = ctx.enter_context(nc.psum_tensor("a_var", [P, G], F32))
        mod = ctx.enter_context(nc.psum_tensor("m_mod", [P, SW], F32))
        s = semaphores(nc, ctx, "k_in k_b_ps k_chain k_sq_rdy k_sq2_rdy k_den k_R_rdy "
                                "k_S_ps k_Z k_F_ps k_K_rdy k_KT_ps k_KT_sb k_out k_strip_in k_strip_ps k_hi "
                                "k_S_rdy k_zero_rdy "
                                "m_in m_exp m_chain m_silu_rdy m_w_used m_rows_rdy m_turned m_spread "
                                "m_slice_rdy "
                                "a_x2_out a_stat_out "
                                "a_hi_rdy a_lo_rdy a_hl_free a_conv_rdy a_x2_rdy "
                                "a_sum1 a_sum2 a_mean1 a_var1 a_mean2 a_var2 "
                                "a_now_rdy a_dev1 a_sq1_rdy a_sqa1 a_sd1 a_rstd1 a_u1 a_h_rdy "
                                "a_dev2 a_sq2_rdy a_sqa2 a_sd2 a_stat_rdy")
        x_in = [semaphores(nc, ctx, " ".join(f"a_x_in{n}{c}" for c in range(NC))) for n in range(2)]
        x_in = [list(d.values()) for d in x_in]
        w1_in = list(semaphores(nc, ctx, " ".join(f"m_w1_in{n}" for n in range(W1_RING))).values())
        w2_in = list(semaphores(nc, ctx, " ".join(f"m_w2_in{n}" for n in range(W2_RING))).values())
        block = ctx.enter_context(nc.Block())
        NK_IN, NM_IN = 11, 5
        NP2 = NB // 2

        @block.sync
        def _(sp):
            def load(group, c):
                g, par, _ = group
                sp.dma_start(X[par][:, c * CB4:(c + 1) * CB4, :],
                             of_group(io["x"], g, c * CB4, CB4)).then_inc(x_in[par][c], 16)

            def store(group, c):
                g, par, _ = group
                sp.wait_ge(s["a_x2_rdy"], NB * g + (c + 1) * CB4)
                sp.dma_start(of_group(io["x2"], g, c * CB4, CB4),
                             X[par][:, c * CB4:(c + 1) * CB4, :]).then_inc(s["a_x2_out"], 16)

            def store_stat(g):
                sp.wait_ge(s["a_stat_rdy"], g + 1)
                sp.dma_start(of_group(io["stat"], g, 0, 2), stat[:]).then_inc(s["a_stat_out"], 16)

            def tiles1(r):
                for k in range(NB):
                    n = NB * r + k
                    if n >= W1_RING:
                        sp.wait_ge(s["m_w_used"], n - W1_RING + 1)
                    for m in range(3):
                        sp.dma_start(w1[m][:, n % W1_RING, :], io["wmod1"][m, r, k]).then_inc(w1_in[n % W1_RING], 16)

            def tiles2(g, ks):
                for k in ks:
                    sp.wait_ge(s["m_w_used"], NW1 + NB * (g - 1) + max(k + 1 - W2_RING, 0))
                    sp.dma_start(w2[:, k % W2_RING, :],
                                 io["wmod2"][bass.ds(g - 1, 1), k, :, :].rearrange("g p c -> (g p) c")
                                 ).then_inc(w2_in[k % W2_RING], 16)

            def step(group):
                g = group[0]
                tiles = not is_last(group)
                if tiles:
                    tiles2(g, range(0, 4))
                store(group, 0)
                for c in range(NC):
                    if tiles:
                        tiles2(g, [4 + c])
                    if not is_last(group):
                        if c == 0:
                            sp.wait_ge(s["a_x2_out"], 16 * NC * g + 16)
                            sp.wait_ge(s["a_sum2"], (NB - 1) * (g - 1) + NB - 1)
                        sp.wait_ge(s["a_dev2"], NP2 * (g - 1) + 2 * (c + 1))
                        load(following(group), c)
                store(group, 1)
                store_stat(g - 1)
                if tiles:
                    tiles2(g, range(8, 13))
                store(group, 2)
                if tiles:
                    tiles2(g, range(13, NB))
                store(group, 3)

            first = (0, 0, 0)
            for dst, src in ((ct[:], io["cT"]), (ident[:], io["ident"]), (bias[:], io["biasT"]),
                             (ones[:], io["ones"]), (epsc[:], io["eps"])):
                sp.dma_start(dst, src).then_inc(s["m_in"], 16)
            for c in range(NC):
                load(first, c)
            tiles1(0)
            tiles1(1)
            sp.wait_ge(s["k_strip_ps"], 1)
            for c in range(NC):
                load(following(first), c)
            tiles1(2)
            store(first, 0)
            tiles1(3)
            for c in range(1, NC):
                store(first, c)
            over_later_groups(sp, step)
            store_stat(NG - 1)
            sp.wait_ge(s["a_x2_out"], 16 * NC * NG)
            sp.wait_ge(s["a_stat_out"], 16 * NG)
            sp.wait_ge(s["k_out"], 32)

        @block.tensor
        def _(pe):
            mm = nc.tensor.matmul


            def state_vectors():
                pe.wait_ge(s["k_in"], 16 * NK_IN)
                mm(conv[:, 4, 0:1], vc[:, 0, :], bp[:, 0:1], start=True, stop=True)
                mm(conv[:, 4, 1:2], vc[:, 1, :], bp[:, 0:1], start=True, stop=True).then_inc(s["k_b_ps"], 1)

            def cauchy_sums():
                pe.wait_ge(s["k_R_rdy"], 1)
                for h in range(2):
                    part = slice(64 * h, 64 * h + 64)
                    for j in range(NB):
                        out = conv[part, 4, 8 + 8 * j:16 + 8 * j]
                        mm(out, kt[4][part, j:KH:NB], V[part, 0, :], start=True, stop=False)
                        last = mm(out, kt[5][part, j:KH:NB], V[part, 1, :], start=False, stop=True)
                last.then_inc(s["k_S_ps"], 1)

            def inverse_dft():
                pe.wait_ge(s["k_Z"], 1)
                out = conv[:, 4, 160:160 + 2 * NB]
                mm(out, idft[:, 0, :], Z1[:].rearrange("p j r -> p (j r)"), start=True, stop=False)
                mm(out, idft[:, 1, :], Z2[:].rearrange("p j r -> p (j r)"), start=False, stop=True
                   ).then_inc(s["k_F_ps"], 1)

            def turn_k():
                pe.wait_ge(s["k_K_rdy"], 1)
                nc.tensor.transpose(conv[0:NB, 4, 256:256 + P], K[:], ident[:]).then_inc(s["k_KT_ps"], 1)

            def flip_strip():
                pe.wait_ge(s["k_strip_in"], 16)
                for n in range(4):
                    last = mm(conv[:, n, :], flip[:], strip[:, n * G:(n + 1) * G], start=True, stop=True)
                last.then_inc(s["k_strip_ps"], 1)


            def tile1(r, k):
                n = NB * r + k
                if k == 0 and r > 0:
                    pe.wait_ge(s["m_spread"], r)
                pe.wait_ge(w1_in[n % W1_RING], 48 * (n // W1_RING + 1))
                for m in range(3):
                    last = mm(mod[32 * m:32 * m + BATCH, :], sl[:, k, :], w1[m][:, n % W1_RING, :],
                              start=(k == 0), stop=(k == NB - 1), tile_position=(0, 32 * m))
                last.then_inc(s["m_w_used"], 1)

            def tile2(g, k):
                if k == 0:
                    pe.wait_ge(s["m_spread"], SLICES + g - 1)
                pe.wait_ge(w2_in[k % W2_RING], 16 * ((NB // W2_RING) * (g - 1) + k // W2_RING + 1))
                q = W2_COLS // 4
                for m in range(4):
                    last = mm(mod[32 * m:32 * m + BATCH, 0:q], sl[:, k, :], w2[:, k % W2_RING, m * q:(m + 1) * q],
                              start=(k == 0), stop=(k == NB - 1), tile_position=(0, 32 * m))
                last.then_inc(s["m_w_used"], 1)

            def turn(rounds, n):
                pe.wait_ge(s["m_rows_rdy"], rounds)
                for k in range(n):
                    last = nc.tensor.transpose(mod[:, k * P:(k + 1) * P], rows[:, k * P:(k + 1) * P], ident[:])
                last.then_inc(s["m_turned"], 1)


            def total(out, acc, rdy, value, sem):
                pe.wait_ge(rdy, value)
                mm(out[:], ones[:], acc[:], start=True, stop=True).then_inc(sem, 1)

            def mean1(g):
                if not (isinstance(g, int) and g <= 1):
                    pe.wait_ge(s["a_stat_rdy"], g - 1)
                total(mean, acc1, s["a_sum1"], (NB - 1) * (g + 1), s["a_mean1"])

            def var1(g):
                total(var, sqa, s["a_sqa1"], (NB - 1) * (g + 1), s["a_var1"])

            def mean2(g):
                total(mean, acc2, s["a_sum2"], (NB - 1) * (g + 1), s["a_mean2"])

            def var2(g):
                total(var, sqa, s["a_sqa2"], (NB - 1) * (g + 1), s["a_var2"])


            def unit(g, j, a):
                if a == 0:
                    pe.wait_ge(s["a_hi_rdy"], NB * g + j + 1)
                    pe.wait_ge(s["a_lo_rdy"], NB * g + j + 1)
                    if j >= CONV_BANKS:
                        pe.wait_ge(s["a_x2_rdy"], NB * g + j - CONV_BANKS + 1)
                    elif not (isinstance(g, int) and g == 0):
                        prev = max(n for n in range(NB) if n % CONV_BANKS == j)
                        pe.wait_ge(s["a_x2_rdy"], NB * g - NB + prev + 1)
                out = conv[:, j % CONV_BANKS, :]
                cols = slice((j - a) * P, (j - a + 1) * P)
                mm(out, S_hi[:, cols], h_hi[:, a, :], start=(a == 0), stop=False)
                mm(out, S_hi[:, cols], h_lo[:, a, :], start=False, stop=False)
                last = mm(out, S_lo[:, cols], h_hi[:, a, :], start=False, stop=(a == j))
                if a == j:
                    last.then_inc(s["a_conv_rdy"], 1)
                elif j == NB - 1:
                    last.then_inc(s["a_hl_free"], 1)

            def step(group):
                g = group[0]
                for u, (j, a) in enumerate(UNITS):
                    if u == AT_MEAN2:
                        mean2(g - 1)
                    if u == AT_VAR2:
                        var2(g - 1)
                    if not is_last(group):
                        if u in AT_TILE:
                            tile2(g, AT_TILE.index(u))
                        if u == AT_MEAN1:
                            mean1(g + 1)
                        if u == AT_VAR1:
                            var1(g + 1)
                        if u == AT_TURN:
                            turn(SLICES + g, TURNS)
                    unit(g, j, a)

            state_vectors()
            pe.wait_ge(s["m_silu_rdy"], 1)
            for k in range(NB):
                tile1(0, k)
                if k == 6:
                    cauchy_sums()
                if k == 8:
                    inverse_dft()
                if k == 9:
                    turn_k()
                if k == 12:
                    mean1(0)
                if k == 13:
                    flip_strip()
            turn(1, SLICE)
            var1(0)
            pe.wait_ge(s["k_S_rdy"], 1)
            for r in range(SLICES):
                units = [x for x in UNITS if x[0] // SLICE == r]
                for n, (j, a) in enumerate(units):
                    if r + 1 < SLICES:
                        for k in range(NB):
                            if k * len(units) // NB == n:
                                tile1(r + 1, k)
                    else:
                        if n == 10:
                            mean1(1)
                        if n == len(units) - 3:
                            var1(1)
                    unit(0, j, a)
                if r + 1 < SLICES:
                    turn(r + 2, SLICE)
            over_later_groups(pe, step)
            mean2(NG - 1)
            var2(NG - 1)

        @block.vector
        def _(dve):
            v = nc.vector
            mul, add, sub = ALU.mult, ALU.add, ALU.subtract
            done = {"k_chain": 0, "m_chain": 0}

            def link(ins, chain="k_chain"):
                done[chain] += 1
                ins.then_inc(s[chain], 1)
                dve.wait_ge(s[chain], done[chain])


            def two_over_step():
                e = lambda n: ex[:, n:n + 1]
                link(v.tensor_scalar(e(0), scal[:, 0:1], -1.0, None, mul))
                link(v.tensor_scalar(e(1), e(0), 1.0 / LN2, ROUND, mul, add))
                link(v.tensor_scalar(e(1), e(1), -ROUND, None, add))
                link(v.scalar_tensor_tensor(e(2), e(1), -LN2_HI, e(0), mul, add))
                link(v.scalar_tensor_tensor(e(2), e(1), -(LN2 - LN2_HI), e(2), mul, add))
                link(v.tensor_scalar(e(3), e(2), 1.0 / math.factorial(8), 1.0 / math.factorial(7), mul, add))
                for n in range(6, -1, -1):
                    link(v.tensor_scalar(e(3), e(3), e(2), 1.0 / math.factorial(n), mul, add))
                link(v.tensor_scalar(e(1), e(1), 127.0, -126.0, ALU.min, ALU.max))
                link(v.tensor_scalar(e(1), e(1), 127.0, 2.0 ** 23, add, mul))
                link(v.tensor_copy(exi[:], e(1)))
                link(v.tensor_tensor(scal[:, 1:2], e(3), exi[:].bitcast(F32), mul))
                link(v.tensor_scalar(scal[:, 2:3], scal[:, 1:2], 2.0, None, mul))

            def resolvents():
                v.tensor_scalar(scal[:, 3:4], st[:, 1:2], -1.0, None, mul)
                link(v.tensor_scalar(scal[:, 4:5], st[:, 0:1], -1.0, None, mul))
                link(v.tensor_scalar(kt[0][:], trig[:, 1, :], scal[:, 2:3], None, mul))
                v.scalar_tensor_tensor(kt[1][:], trig[:, 0, :], scal[:, 3:4], kt[0][:], mul, add).then_inc(s["k_den"], 1)
                dve.wait_ge(s["k_den"], 1)
                dve.wait_ge(s["k_b_ps"], 1)
                link(v.tensor_copy(bvec[:], conv[:, 4, 0:2]))
                U = {"C": (st[:, 6:7], st[:, 7:8]), "q": (st[:, 4:5], st[:, 5:6])}
                Wv = {"B": (bvec[:, 0:1], bvec[:, 1:2]), "p": (st[:, 2:3], st[:, 3:4])}
                for n, (a, b) in enumerate([("C", "B"), ("C", "p"), ("q", "B"), ("q", "p")]):
                    (ur, ui), (wr, wi) = U[a], Wv[b]
                    v.tensor_tensor(pr[:, n, 0:1], ur, wr, mul)
                    v.tensor_tensor(pr[:, n, 1:2], ui, wi, mul)
                    v.tensor_tensor(pr[:, n, 2:3], ur, wi, mul)
                    last = v.tensor_tensor(pr[:, n, 3:4], ui, wr, mul)
                link(last)
                v.tensor_tensor(vv[:, :, 0], pr[:, :, 0], pr[:, :, 1], add)
                link(v.tensor_tensor(vv[:, :, 1], pr[:, :, 2], pr[:, :, 3], sub))
                Vr = V[:].rearrange("p h (n r) -> p h n r", r=2)
                v.tensor_copy(V[:, 0, :], vv[:].rearrange("p n r -> p (n r)"))
                v.tensor_copy(Vr[:, 1, :, 0], vv[:, :, 1])
                v.tensor_scalar(Vr[:, 1, :, 1], vv[:, :, 0], -1.0, None, mul)
                dve.wait_ge(s["k_sq_rdy"], 1)
                dve.wait_ge(s["k_sq2_rdy"], 1)
                link(v.tensor_tensor(kt[2][:], kt[2][:], kt[3][:], add))
                link(v.reciprocal(kt[3][:], kt[2][:]))
                v.scalar_tensor_tensor(kt[4][:], trig[:, 0, :], scal[:, 4:5], kt[3][:], mul, mul)
                v.tensor_tensor(kt[5][:], kt[1][:], kt[3][:], mul).then_inc(s["k_R_rdy"], 1)

            def frequencies():
                dve.wait_ge(s["k_S_ps"], 1)
                link(v.tensor_copy(S8[:].rearrange("p j n -> p (j n)"), conv[:, 4, 8:8 + P]))
                r = lambda n: S8[:, :, 2 * n]
                i = lambda n: S8[:, :, 2 * n + 1]
                T = lambda n: w[:, n, :]
                v.tensor_tensor(T(0), cospj[:], r(3), mul)
                v.tensor_tensor(T(1), cospj[:], i(3), mul)
                v.tensor_tensor(T(2), r(1), r(2), mul)
                v.tensor_tensor(T(3), i(1), i(2), mul)
                v.tensor_tensor(T(4), r(1), i(2), mul)
                link(v.tensor_tensor(T(5), i(1), r(2), mul))
                v.tensor_scalar(T(6), T(0), 1.0, None, add)
                v.tensor_tensor(T(7), T(2), T(3), sub)
                link(v.tensor_tensor(T(8), T(4), T(5), add))
                v.tensor_tensor(T(9), T(6), T(6), mul)
                v.tensor_tensor(T(10), T(1), T(1), mul)
                v.tensor_tensor(T(11), T(7), T(6), mul)
                v.tensor_tensor(T(12), T(8), T(1), mul)
                v.tensor_tensor(T(13), T(8), T(6), mul)
                link(v.tensor_tensor(T(14), T(7), T(1), mul))
                v.tensor_tensor(T(15), T(9), T(10), add)
                v.tensor_tensor(T(16), T(11), T(12), add)
                link(v.tensor_tensor(T(17), T(13), T(14), sub))
                link(v.reciprocal(T(18), T(15)))
                link(v.tensor_tensor(T(19), T(18), cospj[:], mul))
                v.tensor_tensor(T(20), T(16), T(19), mul)
                link(v.tensor_tensor(T(21), T(17), T(19), mul))
                v.tensor_tensor(Z1[:, :, 0], r(0), T(20), sub)
                link(v.tensor_tensor(Z1[:, :, 1], i(0), T(21), sub))
                v.tensor_scalar(Z2[:, :, 0], Z1[:, :, 1], -1.0, None, mul)
                v.tensor_copy(Z2[:, :, 1], Z1[:, :, 0]).then_inc(s["k_Z"], 1)

            def kernel_values():
                dve.wait_ge(s["k_F_ps"], 1)
                link(v.tensor_copy(Fs[:], conv[:, 4, 160:160 + 2 * NB]))
                link(v.tensor_tensor(prod[:], unroll[:], Fs[:].unsqueeze(1).broadcast_to([P, NB, 2 * NB]), mul))
                link(v.tensor_reduce(K[:], prod[:], AX.X, add))
                v.tensor_tensor(K[0:1, 0:1], K[0:1, 0:1], dsb[:], add).then_inc(s["k_K_rdy"], 1)
                dve.wait_ge(s["k_KT_ps"], 1)
                v.tensor_copy(KT[:], conv[0:NB, 4, 256:256 + P]).then_inc(s["k_KT_sb"], 1)

            def strip_low():
                dve.wait_ge(s["k_hi"], 1)
                v.tensor_tensor(S_lo[:], conv[:, 0:4, :].rearrange("p b r -> p (b r)"), S_hi[:], sub
                                ).then_inc(s["k_S_rdy"], 1)


            def collect(rounds, used, n, cols):
                dve.wait_ge(s["m_w_used"], used)
                for m in range(n):
                    last = v.tensor_copy(rows[32 * m:32 * m + BATCH, 0:cols], mod[32 * m:32 * m + BATCH, 0:cols])
                last.then_inc(s["m_rows_rdy"], 1)

            def gate(dst, n):
                a, b = g1[:, :, 0:n], g2[:, :, 0:n]
                mlink = lambda ins: link(ins, "m_chain")
                v.tensor_scalar(a, dst, 0.0, 2.0, ALU.is_ge, mul)
                mlink(v.tensor_scalar(b, dst, -1.0, None, mul))
                v.tensor_scalar(a, a, -1.0, None, add)
                mlink(v.tensor_tensor(b, b, dst, ALU.max))
                mlink(v.tensor_scalar(b, b, 0.25, None, ALU.max))
                mlink(v.tensor_tensor(dst, a, b, mul))

            def slice_scalars(r):
                dve.wait_ge(s["m_turned"], r + 1)
                src = mod[:].rearrange("p (n q c) -> p n q c", n=SLICE, q=4)
                for m in range(3):
                    c0 = m * NB + r * SLICE
                    last = v.tensor_copy(modT[:, :, c0:c0 + SLICE], src[:, :, m, 0:BATCH].rearrange("p n b -> p b n"))
                last.then_inc(s["m_spread"], 1)
                dve.wait_ge(s["m_spread"], r + 1)
                comp = lambda m: modT[:, :, m * NB + r * SLICE:m * NB + (r + 1) * SLICE]
                v.tensor_scalar(comp(CA), comp(CA), 1.0, None, add).then_inc(s["m_slice_rdy"], 1)
                gate(comp(GA), SLICE)

            def sixth_scalars(group):
                g, par, b = group
                i = b if par == 1 else b - 1
                dve.wait_ge(s["m_turned"], SLICES + g)
                src = mod[:, 0:TURNS * P].rearrange("p (n q c) -> p n q c", n=TURNS, q=4)
                for n in range(TURNS):
                    dst = modT[:, :, bass.DynSlice((3 + i) * NB + (0 if par == 1 else NB // 2) + n, 4, TURNS)]
                    last = v.tensor_scalar(dst, src[:, n, :, 0:BATCH].rearrange("p q b -> p b q"), 1.0, None, mul)
                last.then_inc(s["m_spread"], 1)

            def finish_scalars():
                dve.wait_ge(s["m_spread"], SLICES + 6)
                comp = lambda m: modT[:, :, m * NB:(m + 1) * NB]
                v.tensor_scalar(comp(CB), comp(CB), 1.0, None, add)
                gate(comp(GB), NB)
                v.tensor_tensor(comp(GBIAS), comp(GB), bias[:].unsqueeze(1).broadcast_to([P, BATCH, NB]), mul)


            def pair(t, n):
                return t[:, 2 * n:2 * n + 2, :]

            def twice(row):
                return row.unsqueeze(1).broadcast_to([P, 2, G])

            def epilogue(group, *js):
                g, par, b = group
                for j in js:
                    dve.wait_ge(s["a_conv_rdy"], NB * g + j + 1)
                    x = X[par][:, j, :]
                    v.scalar_tensor_tensor(x, conv[:, j % CONV_BANKS, :], scalar_of(modT, b, GA * NB + j), x,
                                           mul, add).then_inc(s["a_x2_rdy"], 1)

            def add_squares(g, n, rdy, chain):
                dve.wait_ge(rdy, NP2 * g + n + 1)
                t = sq[:, n % 2]
                if n == 0:
                    v.tensor_tensor(sqa[:], t[:, 0, :], t[:, 1, :], add).then_inc(chain, 1)
                    return
                base = (NB - 1) * g + 2 * n - 1
                dve.wait_ge(chain, base)
                v.tensor_tensor(sqa[:], sqa[:], t[:, 0, :], add).then_inc(chain, 1)
                dve.wait_ge(chain, base + 1)
                v.tensor_tensor(sqa[:], sqa[:], t[:, 1, :], add).then_inc(chain, 1)

            def variance2(group, ns):
                g, par, _ = group
                for n in ns:
                    if n == 0:
                        dve.wait_ge(s["a_mean2"], g + 1)
                        last1 = min(g + 1, NG - 1) if isinstance(g, int) else g + 1
                        dve.wait_ge(s["a_sqa1"], (NB - 1) * (last1 + 1))
                        dve.wait_ge(s["a_u1"], NP2 * (last1 + 1))
                    if n >= 2:
                        dve.wait_ge(s["a_sqa2"], (NB - 1) * g + 2 * n - 3)
                    v.tensor_tensor(sq[:, n % 2], pair(X[par], n), twice(mean[:]), sub).then_inc(s["a_dev2"], 1)
                    if n > 0:
                        add_squares(g, n - 1, s["a_sq2_rdy"], s["a_sqa2"])
                    if n == NP2 - 1:
                        add_squares(g, n, s["a_sq2_rdy"], s["a_sqa2"])

            def variance1(group, ns):
                g, par, _ = group
                for n in ns:
                    if n == 0:
                        dve.wait_ge(s["a_mean1"], g + 1)
                        if not is_first(group):
                            dve.wait_ge(s["a_lo_rdy"], NB * g)
                    v.tensor_tensor(pair(H, n), pair(X[par], n), twice(mean[:]), sub).then_inc(s["a_dev1"], 1)
                    if n > 0:
                        add_squares(g, n - 1, s["a_sq1_rdy"], s["a_sqa1"])
                    if n == NP2 - 1:
                        add_squares(g, n, s["a_sq1_rdy"], s["a_sqa1"])

            def finish2(g):
                if not (isinstance(g, int) and g == 0):
                    dve.wait_ge(s["a_stat_out"], 16 * g)
                v.tensor_copy(stat[:, 0, :], mean[:])
                dve.wait_ge(s["a_sd2"], g + 1)
                v.reciprocal(stat[:, 1, :], sqa[:]).then_inc(s["a_stat_rdy"], 1)

            def inverse1(group):
                g = group[0]
                dve.wait_ge(s["a_sd1"], g + 1)
                v.reciprocal(sqa[:], sqa[:]).then_inc(s["a_rstd1"], 1)
                dve.wait_ge(s["a_rstd1"], g + 1)

            def scale1(ns):
                for n in ns:
                    v.tensor_tensor(pair(H, n), pair(H, n), twice(sqa[:]), mul).then_inc(s["a_u1"], 1)

            def step(group):
                g, par, b = group
                prev = (g - 1, 1 - par, None)
                nxt = following(group)
                last = is_last(group)
                E = lambda *js: epilogue(group, *js)
                E(0, 1, 2, 3)
                variance2(prev, range(0, 2))
                E(4)
                variance2(prev, range(2, 4))
                E(5)
                variance2(prev, range(4, 6))
                E(6, 7)
                variance2(prev, range(6, 8))
                E(8)
                finish2(g - 1)
                E(9)
                if last:
                    finish_scalars()
                    E(10, 11, 12, 13, 14, 15)
                    return
                variance1(nxt, range(0, 2))
                E(10)
                variance1(nxt, range(2, 4))
                E(11)
                variance1(nxt, range(4, 7))
                E(12)
                variance1(nxt, range(7, 8))
                E(13)
                inverse1(nxt)
                scale1(range(0, 2))
                collect(SLICES + g, NW1 + NB * g, 4, W2_COLS // 4)
                scale1(range(2, 4))
                E(14)
                scale1(range(4, 6))
                sixth_scalars(group)
                scale1(range(6, 8))
                E(15)

            v.memset(zero[:], 0.0).then_inc(s["k_zero_rdy"], 1)
            link(v.memset(rows[:], 0.0), "m_chain")
            dve.wait_ge(s["m_exp"], 1)
            link(v.tensor_scalar(ce[:], ce[:], 1.0, None, add), "m_chain")
            link(v.reciprocal(ce[:], ce[:]), "m_chain")
            v.tensor_tensor(sl[:], ct[:], ce[:], mul).then_inc(s["m_silu_rdy"], 1)
            dve.wait_ge(s["m_silu_rdy"], 1)
            dve.wait_ge(s["k_in"], 16 * NK_IN)
            two_over_step()
            resolvents()
            frequencies()
            kernel_values()
            first = (0, 0, 0)
            variance1(first, range(0, 3))
            strip_low()
            variance1(first, range(3, 8))
            collect(1, NB, 3, SW)
            inverse1(first)
            scale1(range(0, 2))
            slice_scalars(0)
            scale1(range(2, 8))
            for r in range(1, SLICES):
                epilogue(first, *range(SLICE * (r - 1), SLICE * r))
                collect(r + 1, NB * (r + 1), 3, SW)
                slice_scalars(r)
            variance1(following(first), range(0, 3))
            epilogue(first, 12)
            variance1(following(first), range(3, 8))
            epilogue(first, 13)
            inverse1(following(first))
            scale1(range(0, 8))
            epilogue(first, 14, 15)
            over_later_groups(dve, step)
            variance2((NG - 1, 1, None), range(0, 8))
            finish2(NG - 1)

        @block.gpsimd
        def _(pool):
            v = nc.gpsimd

            def sum1(group, loads):
                g, par, _ = group
                if not is_first(group):
                    pool.wait_ge(s["a_mean1"], g)
                for n in range(1, NB):
                    if n == 1 or n % CB4 == 0:
                        pool.wait_ge(x_in[par][n // CB4], 16 * loads)
                    if n == 1:
                        v.tensor_tensor(acc1[:], X[par][:, 0, :], X[par][:, 1, :], ALU.add).then_inc(s["a_sum1"], 1)
                    else:
                        pool.wait_ge(s["a_sum1"], (NB - 1) * g + n - 1)
                        v.tensor_tensor(acc1[:], acc1[:], X[par][:, n, :], ALU.add).then_inc(s["a_sum1"], 1)

            def sum2(group, *js):
                g, par, _ = group
                for j in js:
                    pool.wait_ge(s["a_x2_rdy"], NB * g + j + 1)
                    if j == 0:
                        continue
                    if j == 1:
                        if not is_first(group):
                            pool.wait_ge(s["a_mean2"], g)
                        v.tensor_tensor(acc2[:], X[par][:, 0, :], X[par][:, 1, :], ALU.add).then_inc(s["a_sum2"], 1)
                    else:
                        pool.wait_ge(s["a_sum2"], (NB - 1) * g + j - 1)
                        v.tensor_tensor(acc2[:], acc2[:], X[par][:, j, :], ALU.add).then_inc(s["a_sum2"], 1)

            def low(g, blocks):
                for a in blocks:
                    pool.wait_ge(s["a_hi_rdy"], NB * g + a + 1)
                    v.tensor_tensor(h_lo[:, a, :], H[:, a, :], h_hi[:, a, :], ALU.subtract
                                    ).then_inc(s["a_lo_rdy"], 1)

            def step(group):
                g, par, b = group
                sum2(group, *range(0, 6))
                if not is_last(group):
                    sum1(following(group), b + 2 if par == 1 else b + 1)
                sum2(group, *range(6, NB - 1))
                if not is_last(group):
                    low(g + 1, range(0, 8))
                sum2(group, NB - 1)
                if not is_last(group):
                    low(g + 1, range(8, NB))

            first = (0, 0, 0)
            sum1(first, 1)
            for r in range(SLICES):
                low(0, range(SLICE * r, SLICE * (r + 1)))
                if r < SLICES - 1:
                    sum2(first, *range(SLICE * r, SLICE * (r + 1)))
                if r == 1:
                    sum1(following(first), 1)
            sum2(first, 12, 13, 14)
            low(1, range(0, 8))
            sum2(first, 15)
            low(1, range(8, NB))
            over_later_groups(pool, step)

        @block.scalar
        def _(act):
            def squares1(g):
                for n in range(NP2):
                    act.wait_ge(s["a_dev1"], NP2 * g + n + 1)
                    if n >= 2:
                        act.wait_ge(s["a_sqa1"], (NB - 1) * g + 2 * (n - 2) + 1)
                    nc.scalar.activation(sq[:, n % 2], H[:, 2 * n:2 * n + 2, :], ACT.Square).then_inc(s["a_sq1_rdy"], 1)

            def squares2(g):
                for n in range(NP2):
                    act.wait_ge(s["a_dev2"], NP2 * g + n + 1)
                    nc.scalar.activation(sq[:, n % 2], sq[:, n % 2], ACT.Square).then_inc(s["a_sq2_rdy"], 1)

            def sigma(var_rdy, g, done):
                act.wait_ge(var_rdy, g + 1)
                nc.scalar.activation(sqa[:], var[:], ACT.Sqrt, bias=epsc[:, 0:1]).then_inc(done, 1)

            def high(g, a):
                act.wait_ge(s["a_h_rdy"], NB * g + a + 1)
                if not (isinstance(g, int) and g == 0):
                    if a < NB - 1:
                        act.wait_ge(s["a_hl_free"], (NB - 1) * (g - 1) + a + 1)
                    else:
                        act.wait_ge(s["a_conv_rdy"], NB * g)
                nc.scalar.activation(h_hi[:, a, :], H[:, a, :], ACT.Copy).then_inc(s["a_hi_rdy"], 1)

            def split(g, blocks, t):
                for n, a in enumerate(blocks):
                    act.wait_ge(s["a_u1"], NP2 * g + a // 2 + 1)
                    nc.scalar.activation(H[:, a, :], H[:, a, :], ACT.Identity, scale=t[:, CA * NB + a:CA * NB + a + 1],
                                         bias=t[:, SA * NB + a:SA * NB + a + 1]).then_inc(s["a_h_rdy"], 1)
                    if n:
                        high(g, a - 1)
                high(g, blocks[-1])

            def current(group):
                g, _, b = group
                nc.scalar.activation(now[:].rearrange("p m c -> p (m c)"), entry_of(modT, b, 2 * NB), ACT.Copy
                                     ).then_inc(s["a_now_rdy"], 1)
                act.wait_ge(s["a_now_rdy"], g)

            def prepare(group):
                g = group[0]
                squares1(g)
                sigma(s["a_var1"], g, s["a_sd1"])
                current(group)
                split(g, range(NB), now[:].rearrange("p m c -> p (m c)"))

            def step(group):
                g = group[0]
                squares2(g - 1)
                sigma(s["a_var2"], g - 1, s["a_sd2"])
                if not is_last(group):
                    prepare(following(group))

            for dst, src in ((scal[:, 0:1], io["log_step"].to_broadcast([P, 1])), (st[:], io["state"]),
                             (trig[0:64], io["trig"][0].partition_broadcast(64)),
                             (trig[64:128], io["trig"][1].partition_broadcast(64)),
                             (vc[:], io["vcT"]), (bp[:], io["bp"]), (cospj[:], io["cos_pj"]), (idft[:], io["idft"]),
                             (dsb[:], io["dskip"]), (flip[:], io["flip"]), (unroll[:], io["unroll"])):
                act.dma_start(dst, src).then_inc(s["k_in"], 16)
            act.wait_ge(s["m_in"], 16 * NM_IN)
            nc.scalar.activation(ce[:], ct[:], ACT.Exp, scale=-1.0).then_inc(s["m_exp"], 1)
            act.wait_ge(s["k_zero_rdy"], 1)
            act.dma_start(io["kpad"][0:P].rearrange("(a b) -> a b", a=1), zero[:]).then_inc(s["k_out"], 16)
            act.wait_ge(s["k_in"], 16 * NK_IN)
            nc.scalar.activation(kt[2][:], trig[:, 0, :], ACT.Square, scale=st[:, 0:1]).then_inc(s["k_sq_rdy"], 1)
            act.wait_ge(s["k_den"], 1)
            nc.scalar.activation(kt[3][:], kt[1][:], ACT.Square).then_inc(s["k_sq2_rdy"], 1)
            act.wait_ge(s["k_KT_sb"], 1)
            act.dma_start(io["kpad"][P:P + D].rearrange("(a b) -> a b", a=NB), KT[:]).then_inc(s["k_out"], 16)
            act.wait_ge(s["k_out"], 32)
            src = io["kpad"][1:P + D]
            toeplitz = bass.AP(tensor=src.tensor, offset=src.offset, ap=[[1, P], [1, D]])
            act.dma_start(strip[:], toeplitz).then_inc(s["k_strip_in"], 16)
            act.wait_ge(s["k_strip_ps"], 1)
            nc.scalar.activation(S_hi[:], conv[:, 0:4, :].rearrange("p b r -> p (b r)"), ACT.Copy).then_inc(s["k_hi"], 1)
            squares1(0)
            sigma(s["a_var1"], 0, s["a_sd1"])
            act.wait_ge(s["k_S_rdy"], 1)
            for r in range(SLICES):
                act.wait_ge(s["m_slice_rdy"], r + 1)
                if r == SLICES - 1:
                    act.wait_ge(s["m_w_used"], NW1)
                split(0, range(SLICE * r, SLICE * (r + 1)), modT[:, 0, :])
            prepare((1, 1, 0))
            over_later_groups(act, step)
            squares2(NG - 1)
            sigma(s["a_var2"], NG - 1, s["a_sd2"])




def phase_f(nc, io, keep, half):
    W_hi, W_lo = keep["W_hi"], keep["W_lo"]
    NT = NB * 2
    RING = 4
    with ExitStack() as ctx:
        nm = lambda n: f"f{half}_{n}"
        sb = lambda n, s, d=F32: ctx.enter_context(nc.sbuf_tensor(nm(n), s, d))
        wsc = sb("wsc", [P, 2, ER])
        ws = sb("ws", [P, ER])
        bf = sb("bf", [P, ER, HALF])
        bf_hi = sb("bf_hi", [P, ER, HALF], F32R)
        bf_lo = sb("bf_lo", [P, ER, HALF], F32R)
        A = sb("A", [P, NB, ER, P])
        A_hi = sb("A_hi", [P, 2, ER, P], F32R)
        A_lo = sb("A_lo", [P, 2, ER, P], F32R)
        W = sb("W", [P, RING, G])
        ps = ctx.enter_context(nc.psum_tensor(nm("ps"), [P, BANKS, G], F32))
        sems = {n: ctx.enter_context(nc.semaphore(nm(n))) for n in
                "in A_in ws_rdy bf_sc bf_hi_rdy bf_lo_rdy A_hi_rdy A_lo_rdy ps_rdy sum_rdy hi_rdy lo_rdy".split()}
        W_in = [ctx.enter_context(nc.semaphore(nm(f"W_in{n}"))) for n in range(RING)]
        block = ctx.enter_context(nc.Block())

        @block.sync
        def _(sp):
            sp.dma_start(wsc[:], io["wsc"]).then_inc(sems["in"], 16)
            sp.dma_start(bf[:], io["bf"][half]).then_inc(sems["in"], 16)
            sp.dma_start(A[:], io["A"]).then_inc(sems["A_in"], 16)
            for n in range(NT):
                d, c = divmod(n, 2)
                if n >= RING:
                    sp.wait_ge(sems["hi_rdy"], n - RING + 1)
                    sp.wait_ge(sems["lo_rdy"], n - RING + 1)
                sp.dma_start(W[:, n % RING, :], io["W"][half, d, :, c * G:(c + 1) * G]).then_inc(W_in[n % RING], 16)

        @block.tensor
        def _(pe):
            pe.wait_ge(sems["bf_hi_rdy"], 1)
            pe.wait_ge(sems["bf_lo_rdy"], 1)
            for n in range(NT):
                d, c = divmod(n, 2)
                if c == 0:
                    pe.wait_ge(sems["A_hi_rdy"], d + 1)
                    pe.wait_ge(sems["A_lo_rdy"], d + 1)
                if n >= BANKS:
                    pe.wait_ge(sems["sum_rdy"], n - BANKS + 1)
                out = ps[:, n % BANKS, :]
                for e in range(ER):
                    cols = slice(c * G, (c + 1) * G)
                    nc.tensor.matmul(out, A_hi[:, d % 2, e, :], bf_hi[:, e, cols], start=(e == 0), stop=False)
                    nc.tensor.matmul(out, A_hi[:, d % 2, e, :], bf_lo[:, e, cols], start=False, stop=False)
                    mm = nc.tensor.matmul(out, A_lo[:, d % 2, e, :], bf_hi[:, e, cols], start=False,
                                          stop=(e == ER - 1))
                mm.then_inc(sems["ps_rdy"], 1)

        @block.vector
        def _(dve):
            v = nc.vector
            dve.wait_ge(sems["in"], 32)
            v.tensor_tensor(ws[:], wsc[:, 0, :], wsc[:, 1, :], ALU.mult).then_inc(sems["ws_rdy"], 1)
            dve.wait_ge(sems["ws_rdy"], 1)
            for e in range(ER):
                v.tensor_scalar(bf[:, e, :], bf[:, e, :], ws[:, e:e + 1], None, ALU.mult).then_inc(sems["bf_sc"], 1)
            dve.wait_ge(sems["bf_hi_rdy"], 1)
            v.tensor_tensor(bf_lo[:], bf[:], bf_hi[:], ALU.subtract).then_inc(sems["bf_lo_rdy"], 1)

            def a_low(d):
                dve.wait_ge(sems["A_hi_rdy"], d + 1)
                v.tensor_tensor(A_lo[:, d % 2], A[:, d], A_hi[:, d % 2], ALU.subtract).then_inc(sems["A_lo_rdy"], 1)

            a_low(0)
            a_low(1)
            for n in range(NT):
                d, c = divmod(n, 2)
                dve.wait_ge(sems["ps_rdy"], n + 1)
                dve.wait_ge(W_in[n % RING], 16 * (n // RING + 1))
                v.tensor_tensor(W[:, n % RING, :], W[:, n % RING, :], ps[:, n % BANKS, :],
                                ALU.add).then_inc(sems["sum_rdy"], 1)
                if c == 1 and d + 2 < NB:
                    a_low(d + 2)

        @block.scalar
        def _(act):
            act.wait_ge(sems["bf_sc"], ER)
            nc.scalar.activation(bf_hi[:], bf[:], ACT.Copy).then_inc(sems["bf_hi_rdy"], 1)
            act.wait_ge(sems["A_in"], 16)

            def a_high(d):
                if d >= 2:
                    act.wait_ge(sems["ps_rdy"], 2 * (d - 1))
                nc.scalar.activation(A_hi[:, d % 2], A[:, d], ACT.Copy).then_inc(sems["A_hi_rdy"], 1)

            a_high(0)
            a_high(1)
            for n in range(NT):
                d, c = divmod(n, 2)
                if c == 0 and d >= 1 and d + 1 < NB:
                    a_high(d + 1)
                act.wait_ge(sems["sum_rdy"], n + 1)
                nc.scalar.activation(W_hi[:, d, c * G:(c + 1) * G], W[:, n % RING, :], ACT.Copy
                                     ).then_inc(sems["hi_rdy"], 1)

        @block.gpsimd
        def _(pool):
            for n in range(NT):
                d, c = divmod(n, 2)
                cols = slice(c * G, (c + 1) * G)
                pool.wait_ge(sems["hi_rdy"], n + 1)
                nc.gpsimd.tensor_tensor(W_lo[:, d, cols], W[:, n % RING, :], W_hi[:, d, cols],
                                        ALU.subtract).then_inc(sems["lo_rdy"], 1)




def phase_b(nc, io, keep, half):
    modT, W_hi, W_lo = keep["modT"], keep["W_hi"], keep["W_lo"]
    order = [(HB * (1 - half) + n) % NB for n in range(NB)]
    T_RING, HL_RING, O_RING = 4, 4, 4
    NH = NB // 2
    PART = 4
    AHEAD = 3
    with ExitStack() as ctx:
        nm = lambda n: f"b{half}_{n}"
        sb = lambda n, s, d=F32: ctx.enter_context(nc.sbuf_tensor(nm(n), s, d))
        X2 = sb("x2", [P, NB, G])
        T = sb("t", [P, T_RING, G])
        h_hi = sb("hi", [P, HL_RING, G], F32R)
        h_lo = sb("lo", [P, HL_RING, G], F32R)
        stat = sb("stat", [P, GPB, 2, G])
        O = sb("o", [P, O_RING, G])
        now = sb("now", [P, GPB, (NMOD + 1) * NB])
        ps = ctx.enter_context(nc.psum_tensor(nm("ps"), [P, BANKS, G], F32))
        S = {n: ctx.enter_context(nc.semaphore(nm(n))) for n in
             "now_rdy early_in late_in dev u h_rdy hi_rdy lo_rdy hl_free ps_rdy gated out_rdy".split()}
        stat_in = [ctx.enter_context(nc.semaphore(nm(f"stat_in{n}"))) for n in range(GPB)]
        stored = [ctx.enter_context(nc.semaphore(nm(f"stored{n}"))) for n in range(O_RING)]
        block = ctx.enter_context(nc.Block())

        @block.sync
        def _(sp):
            def load(group, k0, sem):
                for k in range(k0, k0 + NH, PART):
                    sp.dma_start(X2[:, k:k + PART, :], of_group(io["x2"], group[0], order[k], PART)
                                 ).then_inc(sem, 16)

            def load_early(group):
                g, par, _ = group
                sp.dma_start(stat[:, par], of_group(io["stat"], g, 0, 2)).then_inc(stat_in[par], 16)
                load(group, 0, S["early_in"])

            def step(group):
                g = group[0]
                if not is_last(group):
                    sp.wait_ge(S["dev"], NB * g + NH)
                    load_early(following(group))
                for o in range(HB):
                    sp.wait_ge(S["out_rdy"], HB * g + o + 1)
                    sp.dma_start(of_group(io["out"], g, half * HB + o, 1), O[:, o % O_RING:o % O_RING + 1, :]
                                 ).then_inc(stored[o % O_RING], 16)
                if not is_last(group):
                    load(following(group), NH, S["late_in"])

            load_early((0, 0, 0))
            load((0, 0, 0), NH, S["late_in"])
            over_groups(sp, step)
            for n in range(O_RING):
                sp.wait_ge(stored[n], 16 * NG * (HB // O_RING))

        @block.vector
        def _(dve):
            v = nc.vector

            def step(group):
                g, par, b = group
                loads = g // GPB + 1 if isinstance(g, int) else (b + 1)
                for k in range(NB):
                    n = NB * g + k
                    if k == 0:
                        dve.wait_ge(stat_in[par], 16 * loads)
                        dve.wait_ge(S["early_in"], 32 * (g + 1))
                    if k == NH:
                        dve.wait_ge(S["late_in"], 32 * (g + 1))
                    if not (is_first(group) and k < T_RING):
                        dve.wait_ge(S["lo_rdy"], n - T_RING + 1)
                    t = T[:, k % T_RING, :]
                    v.tensor_tensor(t, X2[:, k, :], stat[:, par, 0, :], ALU.subtract).then_inc(S["dev"], 1)
                    dve.wait_ge(S["dev"], n + 1)
                    v.tensor_tensor(t, t, stat[:, par, 1, :], ALU.mult).then_inc(S["u"], 1)

            over_groups(dve, step)

        @block.scalar
        def _(act):
            def modulate(group, k):
                g, par, b = group
                if k == 0:
                    nc.scalar.activation(now[:, par, :], entry_of(modT, b, (NMOD + 1) * NB), ACT.Copy
                                         ).then_inc(S["now_rdy"], 1)
                    act.wait_ge(S["now_rdy"], g + 1)
                act.wait_ge(S["u"], NB * g + k + 1)
                t = T[:, k % T_RING, :]
                nc.scalar.activation(t, t, ACT.Identity, scale=now[:, par, CB * NB + order[k]:CB * NB + order[k] + 1],
                                     bias=now[:, par, SB * NB + order[k]:SB * NB + order[k] + 1]
                                     ).then_inc(S["h_rdy"], 1)

            def high(group, k):
                g = group[0]
                act.wait_ge(S["h_rdy"], NB * g + k + 1)
                if k >= HL_RING:
                    act.wait_ge(S["hl_free"], (NB - 1) * g + k - HL_RING + 1)
                elif k < HL_RING - 1 and not is_first(group):
                    act.wait_ge(S["hl_free"], (NB - 1) * (g - 1) + NB + k - HL_RING + 1)
                elif not is_first(group):
                    act.wait_ge(S["ps_rdy"], HB * g)
                nc.scalar.activation(h_hi[:, k % HL_RING, :], T[:, k % T_RING, :], ACT.Copy).then_inc(S["hi_rdy"], 1)

            def split(group, ks):
                for k in ks:
                    modulate(group, k)
                    high(group, k)

            def gate(group, o):
                g, par, _ = group
                blk = half * HB + o
                act.wait_ge(S["ps_rdy"], HB * g + o + 1)
                if not (is_first(group) and o < O_RING):
                    act.wait_ge(stored[o % O_RING], 16 * ((HB // O_RING) * g + o // O_RING))
                nc.scalar.activation(O[:, o % O_RING, :], ps[:, o, :], ACT.Identity,
                                     scale=now[:, par, GB * NB + blk:GB * NB + blk + 1],
                                     bias=now[:, par, GBIAS * NB + blk:GBIAS * NB + blk + 1]
                                     ).then_inc(S["gated"], 1)

            def step(group):
                split(group, range(AHEAD, NB))
                if not is_last(group):
                    split(following(group), range(AHEAD))
                for o in range(HB):
                    gate(group, o)

            split((0, 0, 0), range(AHEAD))
            over_groups(act, step)

        @block.gpsimd
        def _(pool):
            def low(group, ks):
                for k in ks:
                    pool.wait_ge(S["hi_rdy"], NB * group[0] + k + 1)
                    nc.gpsimd.tensor_tensor(h_lo[:, k % HL_RING, :], T[:, k % T_RING, :], h_hi[:, k % HL_RING, :],
                                            ALU.subtract).then_inc(S["lo_rdy"], 1)

            def step(group):
                low(group, range(AHEAD, NB))
                if not is_last(group):
                    low(following(group), range(AHEAD))
                for o in range(HB):
                    pool.wait_ge(S["gated"], HB * group[0] + o + 1)
                    nc.gpsimd.tensor_tensor(O[:, o % O_RING, :], O[:, o % O_RING, :], X2[:, NH + o, :],
                                            ALU.add).then_inc(S["out_rdy"], 1)

            low((0, 0, 0), range(AHEAD))
            over_groups(pool, step)

        @block.tensor
        def _(pe):
            mm = nc.tensor.matmul

            def step(group):
                g = group[0]
                for k in range(NB):
                    pe.wait_ge(S["hi_rdy"], NB * g + k + 1)
                    pe.wait_ge(S["lo_rdy"], NB * g + k + 1)
                    hi, lo = h_hi[:, k % HL_RING, :], h_lo[:, k % HL_RING, :]
                    for o in range(HB):
                        if k == 0 and not is_first(group):
                            pe.wait_ge(S["gated"], HB * (g - 1) + o + 1)
                        cols = slice(o * P, (o + 1) * P)
                        w_hi, w_lo = W_hi[:, order[k], cols], W_lo[:, order[k], cols]
                        mm(ps[:, o, :], w_hi, hi, start=(k == 0), stop=False)
                        mm(ps[:, o, :], w_hi, lo, start=False, stop=False)
                        last = mm(ps[:, o, :], w_lo, hi, start=False, stop=(k == NB - 1))
                        if k == NB - 1:
                            last.then_inc(S["ps_rdy"], 1)
                    if k < NB - 1:
                        last.then_inc(S["hl_free"], 1)

            over_groups(pe, step)




def build(nc, io):
    with ExitStack() as top:
        sb = lambda ctx, n, s, d=F32: ctx.enter_context(nc.sbuf_tensor(n, s, d))
        keep = {
            "modT": sb(top, "modT", [P, BATCH, (NMOD + 1) * NB]),
            "ones": sb(top, "ones", [P, P]),
            "eps": sb(top, "eps", [P, 1]),
        }
        with ExitStack() as conv:
            keep["S_hi"] = sb(conv, "S_hi", [P, D], F32R)
            keep["S_lo"] = sb(conv, "S_lo", [P, D], F32R)
            phase_a(nc, io, keep)
        with ExitStack() as layer:
            keep["W_hi"] = sb(layer, "W_hi", [P, NB, HALF], F32R)
            keep["W_lo"] = sb(layer, "W_lo", [P, NB, HALF], F32R)
            for half in range(2):
                phase_f(nc, io, keep, half)
                phase_b(nc, io, keep, half)


def shape_tables():
    l = np.arange(D)
    theta = np.pi * l / D
    trig = np.stack([np.cos(theta), np.sin(theta)])
    trig[0, D // 2] = 0.0
    p, j, t1 = np.arange(P), np.arange(NB), np.arange(NB)
    t2 = np.arange(P)
    a = 2 * np.pi * np.outer(p, t2) / P + np.pi * p[:, None] / P
    u = (2 * np.pi * j[None, None, :] * t2[:, None, None] / D + np.pi * j[None, None, :] / D
         + 2 * np.pi * j[None, None, :] * t1[None, :, None] / NB)
    unroll = np.stack([np.cos(u), -np.sin(u)], axis=-1) / D
    return {
        "trig": trig.reshape(2, 2, D // 2).transpose(1, 0, 2),
        "cos_pj": trig[0].reshape(P, NB),
        "idft": np.stack([np.cos(a), np.sin(a)], axis=1),
        "unroll": unroll.reshape(P, NB, 2 * NB),
        "ident": np.eye(P),
        "flip": np.eye(P)[::-1],
        "ones": np.full((P, P), 1.0 / D),
        "eps": np.full((P, 1), EPS),
    }


def kernel(**inputs):
    import concourse.bacc as bacc
    from concourse.bass_utils import run_bass_kernel_spmd

    A = {k.removeprefix("L0_"): np.asarray(v) for k, v in inputs.items()}
    twice = lambda a: np.concatenate([a, a], axis=0)
    state = np.concatenate([A["attn_Lambda_ri"], A["attn_p_ri"], A["attn_q_ri"],
                            A["attn_Ct_ri"].reshape(N_STATE, 2)], axis=1)
    per_row = lambda a: np.repeat(a, NE // a.shape[0]).reshape(ER, P).T
    arrays = {
        "x": A["attn_u"].reshape(NG, G, NB, P).transpose(0, 3, 2, 1),
        "state": twice(state),
        "vcT": np.concatenate([A["attn_Vc_ri"].transpose(1, 2, 0)] * 2, axis=2),
        "bp": A["attn_Bp"],
        "dskip": A["attn_D"].reshape(1, 1),
        "log_step": A["attn_log_step"].reshape(1, 1),
        "cT": A["c"].T.reshape(NB, P, BATCH).transpose(1, 0, 2),
        "wmod1": A["wmod"][:, :3 * D].reshape(NB, P, 3, SLICES, SW).transpose(2, 3, 0, 1, 4),
        "wmod2": A["wmod"][:, 3 * D:].reshape(NB, P, 6, W2_COLS).transpose(2, 0, 1, 3),
        "biasT": A["ffn_bias"].reshape(NB, P).T,
        "W": A["ffn_W"].T.reshape(NB, P, 2, HALF).transpose(2, 0, 1, 3),
        "A": A["ffn_A"].reshape(ER, P, NB, P).transpose(1, 2, 0, 3),
        "bf": A["ffn_Bf"].transpose(0, 2, 1).reshape(ER, P, 2, HALF).transpose(2, 1, 0, 3),
        "wsc": np.stack([per_row(A["ffn_coeffs"]), per_row(A["ffn_scales"])], axis=1),
    }
    arrays.update({n: t.astype(np.float32) for n, t in shape_tables().items()})
    arrays = {n: np.ascontiguousarray(a) for n, a in arrays.items()}

    nc = bacc.Bacc("TRN2", target_bir_lowering=False, num_devices=1)
    io = {n: nc.dram_tensor(f"in_{n}", a.shape, F32, kind="ExternalInput").ap() for n, a in arrays.items()}
    io["out"] = nc.dram_tensor("out", (NG, P, NB, G), F32, kind="ExternalOutput").ap()
    io["x2"] = nc.dram_tensor("x2_scratch", (NG, P, NB, G), F32).ap()
    io["stat"] = nc.dram_tensor("stat_scratch", (NG, P, 2, G), F32).ap()
    io["kpad"] = nc.dram_tensor("k_scratch", (P + D,), F32).ap()
    build(nc, io)
    r = run_bass_kernel_spmd(nc, [{f"in_{n}": a for n, a in arrays.items()}], core_ids=[0])
    out = r.results[0]["out"]
    return np.ascontiguousarray(out.transpose(0, 3, 2, 1)).reshape(BATCH, ROWS // BATCH, D)
```

```python
import math
from contextlib import ExitStack

import numpy as np

import concourse.bass as bass
from concourse import mybir

F32 = mybir.dt.float32
F32R = mybir.dt.float32r
ALU = mybir.AluOpType
ACT = mybir.ActivationFunctionType
AX = mybir.AxisListType

P = 128
D = 2048
ROWS = 4096
BATCH = 4
NB = D // P
G = 512
NG = ROWS // G
GPB = NG // BATCH
N_STATE = 64
NMOD = 6
SA, CA, GA, SB, CB, GB, GBIAS = range(NMOD + 1)
EPS = 1e-5
LN2 = math.log(2.0)
LN2_HI = 355.0 / 512.0
ROUND = 1.5 * 2.0 ** 23

CONV_BANKS = 5
BANKS = 8
NE = 16 * 16
ER = NE // P
HALF = D // 2
HB = HALF // P


def semaphores(nc, ctx, names):
    return {n: ctx.enter_context(nc.semaphore(n)) for n in names.split()}


def scalar_of(t, b, c):
    if isinstance(b, int):
        return t[:, b, c:c + 1]
    return t[:, bass.ds(b, 1), c:c + 1].rearrange("p b c -> p (b c)")


def entry_of(t, b, c, n):
    if isinstance(b, int):
        return t[:, b, c:c + n]
    return t[:, bass.ds(b, 1), c:c + n].rearrange("p b c -> p (b c)")


def of_group(t, g, b0, n):
    return t[bass.ds(g, 1), :, b0:b0 + n, :].rearrange("g p b r -> (g p) b r")


def over_groups(eng, step):
    step((0, 0, 0))
    over_later_groups(eng, step)


def over_later_groups(eng, step):
    with eng.Fori(0, (NG - 2) // 2) as i:
        step((2 * i + 1, 1, i))
        step((2 * i + 2, 0, i + 1))
    step((NG - 1, 1, BATCH - 1))


def following(group):
    g, par, b = group
    if isinstance(g, int):
        return (g + 1, 1 - par, (g + 1) // GPB)
    return (g + 1, 1 - par, b + 1 if par == 1 else b)


def is_first(group):
    return isinstance(group[0], int) and group[0] == 0


def is_last(group):
    return isinstance(group[0], int) and group[0] == NG - 1



NT = NB * 2
NH = NB // 2
T_RING, HL_RING, O_RING = 4, 4, 4
A_RING = 4
W_RING = 7
PART = 2
AHEAD = 3
AT_FIRST = [NT - 10, NT - 8, NT - 6]
AT_LOAD = 4
KB = 1024


def fold_arrays(nc, base):
    at = lambda n, kib, s, d=F32: nc.alloc_sbuf_tensor_at(n, s, d, offset=base + kib * KB)
    return {
        "bf_hi": [at(f"f{h}_bf_hi", 16 * (1 - h), [P, ER, HALF], F32R) for h in range(2)],
        "bf_lo": [at(f"f{h}_bf_lo", 16 * (1 - h) + 8, [P, ER, HALF], F32R) for h in range(2)],
        "bf": at("f_bf", 56, [P, HALF]),
        "A_hi": at("f_A_hi", 60, [P, 2, ER, P], F32R),
        "A_lo": at("f_A_lo", 62, [P, 2, ER, P], F32R),
        "W": [at(f"f_W{n}", kib, [P, G]) for n, kib in enumerate((38, 46, 54, 64, 66, 68, 70))],
        "A": at("f_A", 72, [P, A_RING, ER, P]),
    }


def fold_semaphores(nc, ctx, half):
    names = ("bf_in bf_sc bf_hi_rdy bf_lo_rdy A_hi_rdy A_lo_rdy ps_rdy sum_rdy hi_rdy lo_rdy "
             + " ".join(f"A_in{n}" for n in range(A_RING)) + " " + " ".join(f"W_in{n}" for n in range(W_RING)))
    return {n: ctx.enter_context(nc.semaphore(f"f{half}_{n}")) for n in names.split()}


def load_a(sp, io, L, S, d):
    if d >= A_RING:
        sp.wait_ge(S["A_hi_rdy"], d - A_RING + 1)
        sp.wait_ge(S["A_lo_rdy"], d - A_RING + 1)
    sp.dma_start(L["A"][:, d % A_RING], io["A"][:, d]).then_inc(S[f"A_in{d % A_RING}"], 16)


def load_bf_a(sp, io, L, S, half):
    for d in range(A_RING):
        load_a(sp, io, L, S, d)
    for e in range(ER):
        if e > 0:
            sp.wait_ge(S["bf_lo_rdy"], e)
        sp.dma_start(L["bf"][:], io["bf"][half, :, e, :]).then_inc(S["bf_in"], 16)


def load_w(sp, io, L, S, half, n):
    d, c = divmod(n, 2)
    sp.dma_start(L["W"][n % W_RING][:], io["W"][half, d, :, c * G:(c + 1) * G]).then_inc(S[f"W_in{n % W_RING}"], 16)


def a_high(nc, act, L, S, d):
    act.wait_ge(S[f"A_in{d % A_RING}"], 16 * (d // A_RING + 1))
    if d >= 2:
        act.wait_ge(S["ps_rdy"], 2 * (d - 1))
    nc.scalar.activation(L["A_hi"][:, d % 2], L["A"][:, d % A_RING], ACT.Copy).then_inc(S["A_hi_rdy"], 1)


def a_low(nc, dve, L, S, d):
    dve.wait_ge(S["A_hi_rdy"], d + 1)
    nc.vector.tensor_tensor(L["A_lo"][:, d % 2], L["A"][:, d % A_RING], L["A_hi"][:, d % 2], ALU.subtract
                            ).then_inc(S["A_lo_rdy"], 1)


def bf_high(nc, act, L, S, half):
    for e in range(ER):
        act.wait_ge(S["bf_sc"], e + 1)
        nc.scalar.activation(L["bf_hi"][half][:, e, :], L["bf"][:], ACT.Copy).then_inc(S["bf_hi_rdy"], 1)


def bf_low(nc, dve, L, S, half, fw):
    for e in range(ER):
        dve.wait_ge(S["bf_in"], 16 * (e + 1))
        nc.vector.tensor_scalar(L["bf"][:], L["bf"][:], fw[:, 2, e:e + 1], None, ALU.mult).then_inc(S["bf_sc"], 1)
        dve.wait_ge(S["bf_hi_rdy"], e + 1)
        nc.vector.tensor_tensor(L["bf_lo"][half][:, e, :], L["bf"][:], L["bf_hi"][half][:, e, :], ALU.subtract
                                ).then_inc(S["bf_lo_rdy"], 1)



UNITS = [(j, a) for j in range(NB) for a in range(j + 1)]
NU = len(UNITS)
AT_MEAN2, AT_VAR2, AT_MEAN1, AT_VAR1 = 14, 52, 69, 104
AT_TILE = [10 + 13 * k // 2 for k in range(NB)]
PART_MEAN = 12
AT_PART_MEAN = 84
AT_TURN = 122
SLICES = 4
SLICE = NB // SLICES
SW = SLICE * P
NW1 = SLICES * NB
W1_RING = 8
W1_SHORT = W1_RING // 2
AHEAD1 = [14, 8, 6]
W2_COLS = 3 * D // 6
W2_RING = 2
TURNS = W2_COLS // 4 // P
NC = 4
CB4 = NB // NC
KH = D // 2


def w1_slot(n):
    slot = n % (W1_RING if n < NW1 // 2 else W1_SHORT)
    if n < NW1 // 2:
        return slot, n // W1_RING + 1
    return slot, NW1 // 2 // W1_RING + (n - NW1 // 2) // W1_SHORT + 1


def phase_a(nc, io, keep):
    modT, S_hi, S_lo, ones, epsc = keep["modT"], keep["S_hi"], keep["S_lo"], keep["ones"], keep["eps"]
    L, F0, fw = keep["L"], keep["F0"], keep["fw"]
    with ExitStack() as ctx:
        sb = lambda n, s, d=F32: ctx.enter_context(nc.sbuf_tensor(n, s, d))
        base = nc.sbuf_base
        sb("a_slab", [P, 168 * KB // 4])
        at = lambda n, kib, s, d=F32: nc.alloc_sbuf_tensor_at(n, s, d, offset=base + int(kib * KB))
        X = [at(f"a_x{n}", 64 * n, [P, NB, G]) for n in range(2)]
        H = at("a_h", 32, [P, NB, G])
        h_hi = at("a_h_hi", 96, [P, NB, G], F32R)
        h_lo = at("a_h_lo", 128, [P, NB, G], F32R)
        w2 = at("a_w2", 160, [P, W2_RING, W2_COLS])
        w1 = [[at(f"a_w1{n}{m}", kib + 2 * (n % W1_SHORT), [P, SW]) for m, kib in enumerate(places)]
              for n in range(W1_RING) for places in [((120, 152, 160), (104, 112, 144))[n // W1_SHORT]]]
        trig = at("k_trig", 64, [P, 2, KH])
        kt = [at(f"k_t{n}", 72 + 4 * n, [P, KH]) for n in range(6)]
        strip = at("k_strip", 72, [P, D])
        idft = at("k_idft", 128, [P, 2, P])
        unroll = at("k_unroll", 129, [P, NB, 2 * NB])
        prod = at("k_prod", 131, [P, NB, 2 * NB])
        vc = at("k_vc", 133, [N_STATE, 2, P])
        flip = at("k_flip", 134, [P, P])
        S8 = at("k_S8", 134.5, [P, NB, 8])
        w = at("k_w", 135, [P, 22, NB])
        KT = at("k_KT", 136.5, [NB, P])
        zero = at("k_zero", 137, [1, P])
        st = at("k_state", 138, [P, 8])
        bp = at("k_bp", 138.125, [N_STATE, 1])
        cospj = at("k_cospj", 138.25, [P, NB])
        scal = at("k_scal", 138.375, [P, 8])
        ex = at("k_ex", 138.5, [P, 4])
        exi = at("k_exi", 138.625, [P, 1], mybir.dt.int32)
        bvec = at("k_b", 138.75, [P, 2])
        V = at("k_V", 138.875, [P, 2, 8])
        pr = at("k_pr", 139, [P, 4, 4])
        vv = at("k_vv", 139.125, [P, 4, 2])
        Z1 = at("k_Z1", 139.25, [P, NB, 2])
        Z2 = at("k_Z2", 139.5, [P, NB, 2])
        Fs = at("k_F", 139.75, [P, 2 * NB])
        K = at("k_K", 140, [P, NB])
        dsb = at("k_D", 140.125, [1, 1])

        acc1 = sb("a_acc1", [P, G])
        acc2 = sb("a_acc2", [P, G])
        sqa = sb("a_sqa", [P, G])
        sq = sb("a_sq", [P, 2, 2, G])
        stat = sb("a_stat", [P, 2, G])
        now = sb("a_now", [P, 2, NB])
        ident = sb("m_ident", [P, P])
        rows = sb("m_rows", [P, SW])
        ct = sb("m_c", [P, NB, BATCH])
        ce = sb("m_ce", [P, NB, BATCH])
        sl = sb("m_silu", [P, NB, BATCH])
        bias = sb("m_bias", [P, NB])
        g1, g2 = (t[:].rearrange("p n b -> p (n b)").rearrange("p (b n) -> p b n", b=BATCH) for t in (ct, ce))
        conv = ctx.enter_context(nc.psum_tensor("a_conv", [P, CONV_BANKS, G], F32))
        mean = ctx.enter_context(nc.psum_tensor("a_mean", [P, G], F32))
        var = ctx.enter_context(nc.psum_tensor("a_var", [P, G], F32))
        mod = ctx.enter_context(nc.psum_tensor("m_mod", [P, SW], F32))
        s = semaphores(nc, ctx, "k_in k_b_ps k_chain k_sq_rdy k_sq2_rdy k_den k_R_rdy "
                                "k_S_ps k_Z k_F_ps k_K_rdy k_KT_ps k_KT_sb k_out k_strip_in k_strip_ps k_hi "
                                "k_S_rdy k_zero_rdy "
                                "m_in m_exp m_chain m_silu_rdy m_w_used m_rows_rdy m_turned m_spread "
                                "m_slice_rdy "
                                "a_x2_out a_stat_out "
                                "a_hi_rdy a_lo_rdy a_hl_free a_conv_rdy a_x2_rdy "
                                "a_sum1 a_sum2 a_mean1 a_var1 a_mean2 a_var2 "
                                "a_now_rdy a_dev1 a_sq1_rdy a_sqa1 a_sd1 a_rstd1 a_u1 a_h_rdy "
                                "a_dev2 a_sq2_rdy a_sqa2 a_sd2 a_stat_rdy a_mean2_used a_part_mean a_shift_rdy a_var_rdy")
        x_in = [semaphores(nc, ctx, " ".join(f"a_x_in{n}{c}" for c in range(NC))) for n in range(2)]
        x_in = [list(d.values()) for d in x_in]
        w1_in = list(semaphores(nc, ctx, " ".join(f"m_w1_in{n}" for n in range(W1_RING))).values())
        w2_in = list(semaphores(nc, ctx, " ".join(f"m_w2_in{n}" for n in range(W2_RING))).values())
        block = ctx.enter_context(nc.Block())
        NK_IN, NM_IN = 11, 6
        NP2 = NB // 2

        @block.sync
        def _(sp):
            def load(group, c):
                g, par, _ = group
                sp.dma_start(X[par][:, c * CB4:(c + 1) * CB4, :],
                             of_group(io["x"], g, c * CB4, CB4)).then_inc(x_in[par][c], 16)

            def store(group, c):
                g, par, _ = group
                sp.wait_ge(s["a_x2_rdy"], NB * g + (c + 1) * CB4)
                sp.dma_start(of_group(io["x2"], g, c * CB4, CB4),
                             X[par][:, c * CB4:(c + 1) * CB4, :]).then_inc(s["a_x2_out"], 16)

            def store_stat(g):
                sp.wait_ge(s["a_stat_rdy"], g + 1)
                sp.dma_start(of_group(io["stat"], g, 0, 2), stat[:]).then_inc(s["a_stat_out"], 16)

            def tiles1(r):
                for k in range(NB):
                    n = NB * r + k
                    slot, _ = w1_slot(n)
                    if n >= W1_RING:
                        sp.wait_ge(s["m_w_used"], max(o for o in range(n) if w1_slot(o)[0] == slot) + 1)
                    for m in range(3):
                        sp.dma_start(w1[slot][m][:], io["wmod1"][m, r, k]).then_inc(w1_in[slot], 16)

            def tiles2(g, ks):
                for k in ks:
                    sp.wait_ge(s["m_w_used"], NW1 + NB * (g - 1) + max(k + 1 - W2_RING, 0))
                    sp.dma_start(w2[:, k % W2_RING, :],
                                 io["wmod2"][bass.ds(g - 1, 1), k, :, :].rearrange("g p c -> (g p) c")
                                 ).then_inc(w2_in[k % W2_RING], 16)

            def step(group):
                g = group[0]
                tiles = not is_last(group)
                if tiles:
                    tiles2(g, range(0, 4))
                store(group, 0)
                for c in range(NC):
                    if tiles:
                        tiles2(g, [4 + c])
                    if not is_last(group):
                        if c == 0:
                            sp.wait_ge(s["a_x2_out"], 16 * NC * g + 16)
                            sp.wait_ge(s["a_sum2"], (NB - 1) * (g - 1) + NB - 1)
                        sp.wait_ge(s["a_dev2"], NP2 * (g - 1) + 2 * (c + 1))
                        load(following(group), c)
                store(group, 1)
                store_stat(g - 1)
                if is_last(group):
                    sp.wait_ge(s["a_lo_rdy"], NB * NG)
                    sp.wait_ge(s["a_x2_out"], 16 * (NC * g + 2))
                    sp.wait_ge(s["a_sum2"], (NB - 1) * g)
                    sp.wait_ge(s["a_dev2"], NP2 * g)
                    load_bf_a(sp, io, L, F0, 0)
                    for n in range(W_RING):
                        load_w(sp, io, L, F0, 0, n)
                if tiles:
                    tiles2(g, range(8, 13))
                store(group, 2)
                if tiles:
                    tiles2(g, range(13, NB))
                store(group, 3)

            first = (0, 0, 0)
            for dst, src in ((ct[:], io["cT"]), (ident[:], io["ident"]), (bias[:], io["biasT"]),
                             (ones[:], io["ones"]), (epsc[:], io["eps"]), (fw[:, 0:2, :], io["wsc"])):
                sp.dma_start(dst, src).then_inc(s["m_in"], 16)
            for c in range(NC):
                load(first, c)
            tiles1(0)
            tiles1(1)
            sp.wait_ge(s["k_strip_ps"], 1)
            for c in range(NC):
                load(following(first), c)
            tiles1(2)
            store(first, 0)
            tiles1(3)
            for c in range(1, NC):
                store(first, c)
            over_later_groups(sp, step)
            store_stat(NG - 1)
            sp.wait_ge(s["a_x2_out"], 16 * NC * NG)
            sp.wait_ge(s["a_stat_out"], 16 * NG)
            sp.wait_ge(s["k_out"], 32)

        @block.tensor
        def _(pe):
            mm = nc.tensor.matmul


            def state_vectors():
                pe.wait_ge(s["k_in"], 16 * NK_IN)
                mm(conv[:, 4, 0:1], vc[:, 0, :], bp[:, 0:1], start=True, stop=True)
                mm(conv[:, 4, 1:2], vc[:, 1, :], bp[:, 0:1], start=True, stop=True).then_inc(s["k_b_ps"], 1)

            def cauchy_sums():
                pe.wait_ge(s["k_R_rdy"], 1)
                for h in range(2):
                    part = slice(64 * h, 64 * h + 64)
                    for j in range(NB):
                        out = conv[part, 4, 8 + 8 * j:16 + 8 * j]
                        mm(out, kt[4][part, j:KH:NB], V[part, 0, :], start=True, stop=False)
                        last = mm(out, kt[5][part, j:KH:NB], V[part, 1, :], start=False, stop=True)
                last.then_inc(s["k_S_ps"], 1)

            def inverse_dft():
                pe.wait_ge(s["k_Z"], 1)
                out = conv[:, 4, 160:160 + 2 * NB]
                mm(out, idft[:, 0, :], Z1[:].rearrange("p j r -> p (j r)"), start=True, stop=False)
                mm(out, idft[:, 1, :], Z2[:].rearrange("p j r -> p (j r)"), start=False, stop=True
                   ).then_inc(s["k_F_ps"], 1)

            def turn_k():
                pe.wait_ge(s["k_K_rdy"], 1)
                nc.tensor.transpose(conv[0:NB, 4, 256:256 + P], K[:], ident[:]).then_inc(s["k_KT_ps"], 1)

            def flip_strip():
                pe.wait_ge(s["k_strip_in"], 16)
                for n in range(4):
                    last = mm(conv[:, n, :], flip[:], strip[:, n * G:(n + 1) * G], start=True, stop=True)
                last.then_inc(s["k_strip_ps"], 1)


            def tile1(r, k):
                n = NB * r + k
                if k == 0 and r > 0:
                    pe.wait_ge(s["m_spread"], r)
                slot, fills = w1_slot(n)
                pe.wait_ge(w1_in[slot], 48 * fills)
                for m in range(3):
                    last = mm(mod[32 * m:32 * m + BATCH, :], sl[:, k, :], w1[slot][m][:],
                              start=(k == 0), stop=(k == NB - 1), tile_position=(0, 32 * m))
                last.then_inc(s["m_w_used"], 1)

            def tile2(g, k):
                if k == 0:
                    pe.wait_ge(s["m_spread"], SLICES + g - 1)
                pe.wait_ge(w2_in[k % W2_RING], 16 * ((NB // W2_RING) * (g - 1) + k // W2_RING + 1))
                q = W2_COLS // 4
                for m in range(4):
                    last = mm(mod[32 * m:32 * m + BATCH, 0:q], sl[:, k, :], w2[:, k % W2_RING, m * q:(m + 1) * q],
                              start=(k == 0), stop=(k == NB - 1), tile_position=(0, 32 * m))
                last.then_inc(s["m_w_used"], 1)

            def turn(rounds, n):
                pe.wait_ge(s["m_rows_rdy"], rounds)
                for k in range(n):
                    last = nc.tensor.transpose(mod[:, k * P:(k + 1) * P], rows[:, k * P:(k + 1) * P], ident[:])
                last.then_inc(s["m_turned"], 1)


            def total(out, acc, rdy, value, sem):
                pe.wait_ge(rdy, value)
                mm(out[:], ones[:], acc[:], start=True, stop=True).then_inc(sem, 1)

            def mean1(g):
                if not (isinstance(g, int) and g <= 1):
                    pe.wait_ge(s["a_mean2_used"], g - 1)
                total(mean, acc1, s["a_sum1"], (NB - 1) * (g + 1), s["a_mean1"])

            def var1(g):
                if not (isinstance(g, int) and g <= 1):
                    pe.wait_ge(s["a_sd2"], g - 1)
                total(var, sqa, s["a_sqa1"], (NB - 1) * (g + 1), s["a_var1"])

            def mean2(g):
                total(mean, acc2, s["a_sum2"], (NB - 1) * (g + 1), s["a_mean2"])

            def var2(g):
                total(var, sqa, s["a_sqa2"], (NB - 1) * (g + 1), s["a_var2"])


            def unit(g, j, a):
                if a == 0:
                    pe.wait_ge(s["a_hi_rdy"], NB * g + j + 1)
                    pe.wait_ge(s["a_lo_rdy"], NB * g + j + 1)
                    if j >= CONV_BANKS:
                        pe.wait_ge(s["a_x2_rdy"], NB * g + j - CONV_BANKS + 1)
                    elif not (isinstance(g, int) and g == 0):
                        prev = max(n for n in range(NB) if n % CONV_BANKS == j)
                        pe.wait_ge(s["a_x2_rdy"], NB * g - NB + prev + 1)
                out = conv[:, j % CONV_BANKS, :]
                cols = slice((j - a) * P, (j - a + 1) * P)
                mm(out, S_hi[:, cols], h_hi[:, a, :], start=(a == 0), stop=False)
                mm(out, S_hi[:, cols], h_lo[:, a, :], start=False, stop=False)
                last = mm(out, S_lo[:, cols], h_hi[:, a, :], start=False, stop=(a == j))
                if a == j:
                    last.then_inc(s["a_conv_rdy"], 1)
                elif j == NB - 1:
                    last.then_inc(s["a_hl_free"], 1)

            def step(group):
                g = group[0]
                for u, (j, a) in enumerate(UNITS):
                    if u == AT_MEAN2:
                        mean2(g - 1)
                    if u == AT_VAR2:
                        var2(g - 1)
                    if not is_last(group):
                        if u in AT_TILE:
                            tile2(g, AT_TILE.index(u))
                        if u == AT_MEAN1:
                            mean1(g + 1)
                        if u == AT_VAR1:
                            var1(g + 1)
                        if u == AT_TURN:
                            turn(SLICES + g, TURNS)
                    elif u == AT_PART_MEAN:
                        total(mod, acc2, s["a_sum2"], (NB - 1) * g + PART_MEAN - 1, s["a_part_mean"])
                    unit(g, j, a)

            state_vectors()
            pe.wait_ge(s["m_silu_rdy"], 1)
            for k in range(NB):
                tile1(0, k)
                if k == 6:
                    mean1(0)
                if k == 8:
                    cauchy_sums()
            inverse_dft()
            turn_k()
            turn(1, SLICE)
            for k in range(0, 8):
                tile1(1, k)
            flip_strip()
            var1(0)
            for k in range(8, AHEAD1[0]):
                tile1(1, k)
            pe.wait_ge(s["k_S_rdy"], 1)
            for r in range(SLICES):
                units = [x for x in UNITS if x[0] // SLICE == r]
                if 0 < r < SLICES - 1:
                    for k in range(AHEAD1[r]):
                        tile1(r + 1, k)
                for n, (j, a) in enumerate(units):
                    if r + 1 < SLICES:
                        first_k = AHEAD1[r]
                        for k in range(first_k, NB):
                            if (k - first_k) * (len(units) - 6) // (NB - first_k) == n:
                                tile1(r + 1, k)
                    else:
                        if n == 2:
                            mean1(1)
                        if n == 34:
                            var1(1)
                    if r + 1 < SLICES and n == len(units) - 3:
                        turn(r + 2, SLICE)
                    unit(0, j, a)
            over_later_groups(pe, step)
            mean2(NG - 1)
            var2(NG - 1)

        @block.vector
        def _(dve):
            v = nc.vector
            mul, add, sub = ALU.mult, ALU.add, ALU.subtract
            done = {"k_chain": 0, "m_chain": 0}

            def link(ins, chain="k_chain"):
                done[chain] += 1
                ins.then_inc(s[chain], 1)
                dve.wait_ge(s[chain], done[chain])


            def two_over_step():
                e = lambda n: ex[:, n:n + 1]
                link(v.tensor_scalar(e(0), scal[:, 0:1], -1.0, None, mul))
                link(v.tensor_scalar(e(1), e(0), 1.0 / LN2, ROUND, mul, add))
                link(v.tensor_scalar(e(1), e(1), -ROUND, None, add))
                link(v.scalar_tensor_tensor(e(2), e(1), -LN2_HI, e(0), mul, add))
                link(v.scalar_tensor_tensor(e(2), e(1), -(LN2 - LN2_HI), e(2), mul, add))
                link(v.tensor_scalar(e(3), e(2), 1.0 / math.factorial(8), 1.0 / math.factorial(7), mul, add))
                for n in range(6, -1, -1):
                    link(v.tensor_scalar(e(3), e(3), e(2), 1.0 / math.factorial(n), mul, add))
                link(v.tensor_scalar(e(1), e(1), 127.0, -126.0, ALU.min, ALU.max))
                link(v.tensor_scalar(e(1), e(1), 127.0, 2.0 ** 23, add, mul))
                link(v.tensor_copy(exi[:], e(1)))
                link(v.tensor_tensor(scal[:, 1:2], e(3), exi[:].bitcast(F32), mul))
                link(v.tensor_scalar(scal[:, 2:3], scal[:, 1:2], 2.0, None, mul))

            def resolvents():
                v.tensor_scalar(scal[:, 3:4], st[:, 1:2], -1.0, None, mul)
                link(v.tensor_scalar(scal[:, 4:5], st[:, 0:1], -1.0, None, mul))
                link(v.tensor_scalar(kt[0][:], trig[:, 1, :], scal[:, 2:3], None, mul))
                v.scalar_tensor_tensor(kt[1][:], trig[:, 0, :], scal[:, 3:4], kt[0][:], mul, add).then_inc(s["k_den"], 1)
                dve.wait_ge(s["k_den"], 1)
                dve.wait_ge(s["k_b_ps"], 1)
                link(v.tensor_copy(bvec[:], conv[:, 4, 0:2]))
                U = {"C": (st[:, 6:7], st[:, 7:8]), "q": (st[:, 4:5], st[:, 5:6])}
                Wv = {"B": (bvec[:, 0:1], bvec[:, 1:2]), "p": (st[:, 2:3], st[:, 3:4])}
                for n, (a, b) in enumerate([("C", "B"), ("C", "p"), ("q", "B"), ("q", "p")]):
                    (ur, ui), (wr, wi) = U[a], Wv[b]
                    v.tensor_tensor(pr[:, n, 0:1], ur, wr, mul)
                    v.tensor_tensor(pr[:, n, 1:2], ui, wi, mul)
                    v.tensor_tensor(pr[:, n, 2:3], ur, wi, mul)
                    last = v.tensor_tensor(pr[:, n, 3:4], ui, wr, mul)
                link(last)
                v.tensor_tensor(vv[:, :, 0], pr[:, :, 0], pr[:, :, 1], add)
                link(v.tensor_tensor(vv[:, :, 1], pr[:, :, 2], pr[:, :, 3], sub))
                Vr = V[:].rearrange("p h (n r) -> p h n r", r=2)
                v.tensor_copy(V[:, 0, :], vv[:].rearrange("p n r -> p (n r)"))
                v.tensor_copy(Vr[:, 1, :, 0], vv[:, :, 1])
                v.tensor_scalar(Vr[:, 1, :, 1], vv[:, :, 0], -1.0, None, mul)
                dve.wait_ge(s["k_sq_rdy"], 1)
                dve.wait_ge(s["k_sq2_rdy"], 1)
                link(v.tensor_tensor(kt[2][:], kt[2][:], kt[3][:], add))
                link(v.reciprocal(kt[3][:], kt[2][:]))
                v.scalar_tensor_tensor(kt[4][:], trig[:, 0, :], scal[:, 4:5], kt[3][:], mul, mul)
                v.tensor_tensor(kt[5][:], kt[1][:], kt[3][:], mul).then_inc(s["k_R_rdy"], 1)

            def frequencies():
                dve.wait_ge(s["k_S_ps"], 1)
                link(v.tensor_copy(S8[:].rearrange("p j n -> p (j n)"), conv[:, 4, 8:8 + P]))
                r = lambda n: S8[:, :, 2 * n]
                i = lambda n: S8[:, :, 2 * n + 1]
                T = lambda n: w[:, n, :]
                v.tensor_tensor(T(0), cospj[:], r(3), mul)
                v.tensor_tensor(T(1), cospj[:], i(3), mul)
                v.tensor_tensor(T(2), r(1), r(2), mul)
                v.tensor_tensor(T(3), i(1), i(2), mul)
                v.tensor_tensor(T(4), r(1), i(2), mul)
                link(v.tensor_tensor(T(5), i(1), r(2), mul))
                v.tensor_scalar(T(6), T(0), 1.0, None, add)
                v.tensor_tensor(T(7), T(2), T(3), sub)
                link(v.tensor_tensor(T(8), T(4), T(5), add))
                v.tensor_tensor(T(9), T(6), T(6), mul)
                v.tensor_tensor(T(10), T(1), T(1), mul)
                v.tensor_tensor(T(11), T(7), T(6), mul)
                v.tensor_tensor(T(12), T(8), T(1), mul)
                v.tensor_tensor(T(13), T(8), T(6), mul)
                link(v.tensor_tensor(T(14), T(7), T(1), mul))
                v.tensor_tensor(T(15), T(9), T(10), add)
                v.tensor_tensor(T(16), T(11), T(12), add)
                link(v.tensor_tensor(T(17), T(13), T(14), sub))
                link(v.reciprocal(T(18), T(15)))
                link(v.tensor_tensor(T(19), T(18), cospj[:], mul))
                v.tensor_tensor(T(20), T(16), T(19), mul)
                link(v.tensor_tensor(T(21), T(17), T(19), mul))
                v.tensor_tensor(Z1[:, :, 0], r(0), T(20), sub)
                link(v.tensor_tensor(Z1[:, :, 1], i(0), T(21), sub))
                v.tensor_scalar(Z2[:, :, 0], Z1[:, :, 1], -1.0, None, mul)
                v.tensor_copy(Z2[:, :, 1], Z1[:, :, 0]).then_inc(s["k_Z"], 1)

            def kernel_values():
                dve.wait_ge(s["k_F_ps"], 1)
                link(v.tensor_copy(Fs[:], conv[:, 4, 160:160 + 2 * NB]))
                link(v.tensor_tensor(prod[:], unroll[:], Fs[:].unsqueeze(1).broadcast_to([P, NB, 2 * NB]), mul))
                link(v.tensor_reduce(K[:], prod[:], AX.X, add))
                v.tensor_tensor(K[0:1, 0:1], K[0:1, 0:1], dsb[:], add).then_inc(s["k_K_rdy"], 1)
                dve.wait_ge(s["k_KT_ps"], 1)
                v.tensor_copy(KT[:], conv[0:NB, 4, 256:256 + P]).then_inc(s["k_KT_sb"], 1)

            def strip_low():
                dve.wait_ge(s["k_hi"], 1)
                v.tensor_tensor(S_lo[:], conv[:, 0:4, :].rearrange("p b r -> p (b r)"), S_hi[:], sub
                                ).then_inc(s["k_S_rdy"], 1)


            def collect(rounds, used, n, cols):
                dve.wait_ge(s["m_w_used"], used)
                for m in range(n):
                    last = v.tensor_copy(rows[32 * m:32 * m + BATCH, 0:cols], mod[32 * m:32 * m + BATCH, 0:cols])
                last.then_inc(s["m_rows_rdy"], 1)

            def gate(dst, n):
                a, b = g1[:, :, 0:n], g2[:, :, 0:n]
                mlink = lambda ins: link(ins, "m_chain")
                v.tensor_scalar(a, dst, 0.0, 2.0, ALU.is_ge, mul)
                mlink(v.tensor_scalar(b, dst, -1.0, None, mul))
                v.tensor_scalar(a, a, -1.0, None, add)
                mlink(v.tensor_tensor(b, b, dst, ALU.max))
                mlink(v.tensor_scalar(b, b, 0.25, None, ALU.max))
                mlink(v.tensor_tensor(dst, a, b, mul))

            def slice_scalars(r):
                dve.wait_ge(s["m_turned"], r + 1)
                src = mod[:].rearrange("p (n q c) -> p n q c", n=SLICE, q=4)
                for m in range(3):
                    c0 = m * NB + r * SLICE
                    last = v.tensor_copy(modT[:, :, c0:c0 + SLICE], src[:, :, m, 0:BATCH].rearrange("p n b -> p b n"))
                last.then_inc(s["m_spread"], 1)
                dve.wait_ge(s["m_spread"], r + 1)
                comp = lambda m: modT[:, :, m * NB + r * SLICE:m * NB + (r + 1) * SLICE]
                v.tensor_scalar(comp(CA), comp(CA), 1.0, None, add).then_inc(s["m_slice_rdy"], 1)
                gate(comp(GA), SLICE)

            def sixth_scalars(group):
                g, par, b = group
                i = b if par == 1 else b - 1
                dve.wait_ge(s["m_turned"], SLICES + g)
                src = mod[:, 0:TURNS * P].rearrange("p (n q c) -> p n q c", n=TURNS, q=4)
                for n in range(TURNS):
                    dst = modT[:, :, bass.DynSlice((3 + i) * NB + (0 if par == 1 else NB // 2) + n, 4, TURNS)]
                    last = v.tensor_scalar(dst, src[:, n, :, 0:BATCH].rearrange("p q b -> p b q"), 1.0, None, mul)
                last.then_inc(s["m_spread"], 1)

            def finish_scalars():
                dve.wait_ge(s["m_spread"], SLICES + 6)
                comp = lambda m: modT[:, :, m * NB:(m + 1) * NB]
                v.tensor_scalar(comp(CB), comp(CB), 1.0, None, add)
                gate(comp(GB), NB)
                v.tensor_tensor(comp(GBIAS), comp(GB), bias[:].unsqueeze(1).broadcast_to([P, BATCH, NB]), mul)


            def pair(t, n):
                return t[:, 2 * n:2 * n + 2, :]

            def twice(row):
                return row.unsqueeze(1).broadcast_to([P, 2, G])

            def epilogue(group, *js):
                g, par, b = group
                for j in js:
                    dve.wait_ge(s["a_conv_rdy"], NB * g + j + 1)
                    x = X[par][:, j, :]
                    v.scalar_tensor_tensor(x, conv[:, j % CONV_BANKS, :], scalar_of(modT, b, GA * NB + j), x,
                                           mul, add).then_inc(s["a_x2_rdy"], 1)

            def add_squares(g, n, rdy, chain):
                dve.wait_ge(rdy, NP2 * g + n + 1)
                t = sq[:, n % 2]
                if n == 0:
                    v.tensor_tensor(sqa[:], t[:, 0, :], t[:, 1, :], add).then_inc(chain, 1)
                    return
                base = (NB - 1) * g + 2 * n - 1
                dve.wait_ge(chain, base)
                v.tensor_tensor(sqa[:], sqa[:], t[:, 0, :], add).then_inc(chain, 1)
                dve.wait_ge(chain, base + 1)
                v.tensor_tensor(sqa[:], sqa[:], t[:, 1, :], add).then_inc(chain, 1)

            def variance2(group, ns, centre=mean, rdy="a_mean2"):
                g, par, _ = group
                for n in ns:
                    if n == 0:
                        dve.wait_ge(s[rdy], g + 1 if rdy == "a_mean2" else 1)
                        last1 = min(g + 1, NG - 1) if isinstance(g, int) else g + 1
                        dve.wait_ge(s["a_sqa1"], (NB - 1) * (last1 + 1))
                        dve.wait_ge(s["a_u1"], NP2 * (last1 + 1))
                    if n >= 2:
                        dve.wait_ge(s["a_sqa2"], (NB - 1) * g + 2 * n - 3)
                    if rdy == "a_shift_rdy":
                        dve.wait_ge(s["a_x2_rdy"], NB * g + 2 * n + 2)
                    v.tensor_tensor(sq[:, n % 2], pair(X[par], n), twice(centre[:]), sub).then_inc(s["a_dev2"], 1)
                    if n > 0:
                        add_squares(g, n - 1, s["a_sq2_rdy"], s["a_sqa2"])
                    if n == NP2 - 1:
                        add_squares(g, n, s["a_sq2_rdy"], s["a_sqa2"])

            def variance1(group, ns):
                g, par, _ = group
                for n in ns:
                    if n == 0:
                        dve.wait_ge(s["a_mean1"], g + 1)
                        if not is_first(group):
                            dve.wait_ge(s["a_lo_rdy"], NB * g)
                    v.tensor_tensor(pair(H, n), pair(X[par], n), twice(mean[:]), sub).then_inc(s["a_dev1"], 1)
                    if n > 0:
                        add_squares(g, n - 1, s["a_sq1_rdy"], s["a_sqa1"])
                    if n == NP2 - 1:
                        add_squares(g, n, s["a_sq1_rdy"], s["a_sqa1"])

            def provisional():
                dve.wait_ge(s["a_mean1"], NG)
                dve.wait_ge(s["a_part_mean"], 1)
                v.tensor_scalar(acc1[:], mod[:], NB / PART_MEAN, None, mul).then_inc(s["a_shift_rdy"], 1)

            def corrected():
                dve.wait_ge(s["a_mean2"], NG)
                link(v.tensor_tensor(acc1[:], mean[:], acc1[:], sub), "m_chain")
                link(v.tensor_tensor(acc1[:], acc1[:], acc1[:], mul), "m_chain")
                dve.wait_ge(s["a_var2"], NG)
                v.tensor_tensor(acc1[:], var[:], acc1[:], sub).then_inc(s["a_var_rdy"], 1)

            def finish2(g):
                if not (isinstance(g, int) and g == 0):
                    dve.wait_ge(s["a_stat_out"], 16 * g)
                v.tensor_copy(stat[:, 0, :], mean[:]).then_inc(s["a_mean2_used"], 1)
                dve.wait_ge(s["a_sd2"], g + 1)
                v.reciprocal(stat[:, 1, :], sqa[:]).then_inc(s["a_stat_rdy"], 1)

            def inverse1(group):
                g = group[0]
                dve.wait_ge(s["a_sd1"], g + 1)
                v.reciprocal(sqa[:], sqa[:]).then_inc(s["a_rstd1"], 1)
                dve.wait_ge(s["a_rstd1"], g + 1)

            def scale1(ns):
                for n in ns:
                    v.tensor_tensor(pair(H, n), pair(H, n), twice(sqa[:]), mul).then_inc(s["a_u1"], 1)

            def step(group):
                g, par, b = group
                prev = (g - 1, 1 - par, None)
                nxt = following(group)
                last = is_last(group)
                E = lambda *js: epilogue(group, *js)
                E(0, 1, 2, 3)
                variance2(prev, range(0, 2))
                E(4)
                variance2(prev, range(2, 4))
                E(5)
                variance2(prev, range(4, 6))
                E(6, 7)
                variance2(prev, range(6, 8))
                E(8)
                finish2(g - 1)
                E(9)
                if last:
                    finish_scalars()
                    E(10)
                    dve.wait_ge(s["m_in"], 16 * NM_IN)
                    link(v.tensor_tensor(fw[:, 2, :], fw[:, 0, :], fw[:, 1, :], mul), "m_chain")
                    bf_low(nc, dve, L, F0, 0, fw)
                    for d in range(2):
                        a_low(nc, dve, L, F0, d)
                    E(11)
                    provisional()
                    late = lambda ns: variance2(group, ns, acc1, "a_shift_rdy")
                    late(range(0, 2))
                    E(12)
                    late(range(2, 4))
                    E(13)
                    late(range(4, 7))
                    E(14, 15)
                    late(range(7, 8))
                    return
                variance1(nxt, range(0, 2))
                E(10)
                variance1(nxt, range(2, 4))
                E(11)
                variance1(nxt, range(4, 7))
                E(12)
                variance1(nxt, range(7, 8))
                E(13)
                inverse1(nxt)
                scale1(range(0, 2))
                collect(SLICES + g, NW1 + NB * g, 4, W2_COLS // 4)
                scale1(range(2, 4))
                E(14)
                scale1(range(4, 6))
                sixth_scalars(group)
                scale1(range(6, 8))
                E(15)

            v.memset(zero[:], 0.0).then_inc(s["k_zero_rdy"], 1)
            link(v.memset(rows[:], 0.0), "m_chain")
            dve.wait_ge(s["m_exp"], 1)
            link(v.tensor_scalar(ce[:], ce[:], 1.0, None, add), "m_chain")
            link(v.reciprocal(ce[:], ce[:]), "m_chain")
            v.tensor_tensor(sl[:], ct[:], ce[:], mul).then_inc(s["m_silu_rdy"], 1)
            dve.wait_ge(s["m_silu_rdy"], 1)
            dve.wait_ge(s["k_in"], 16 * NK_IN)
            first = (0, 0, 0)
            two_over_step()
            resolvents()
            variance1(first, range(0, 5))
            frequencies()
            kernel_values()
            collect(1, NB, 3, SW)
            variance1(first, range(5, 6))
            slice_scalars(0)
            variance1(first, range(6, 8))
            strip_low()
            inverse1(first)
            scale1(range(0, 8))
            for r in range(1, SLICES):
                epilogue(first, *range(SLICE * (r - 1), SLICE * r - 1))
                collect(r + 1, NB * (r + 1), 3, SW)
                slice_scalars(r)
                epilogue(first, SLICE * r - 1)
            variance1(following(first), range(0, 8))
            epilogue(first, 12)
            inverse1(following(first))
            scale1(range(0, 4))
            epilogue(first, 13)
            scale1(range(4, 8))
            epilogue(first, 14, 15)
            over_later_groups(dve, step)
            corrected()
            finish2(NG - 1)

        @block.gpsimd
        def _(pool):
            v = nc.gpsimd

            def sum1(group, loads):
                g, par, _ = group
                if not is_first(group):
                    pool.wait_ge(s["a_mean1"], g)
                for n in range(1, NB):
                    if n == 1 or n % CB4 == 0:
                        pool.wait_ge(x_in[par][n // CB4], 16 * loads)
                    if n == 1:
                        v.tensor_tensor(acc1[:], X[par][:, 0, :], X[par][:, 1, :], ALU.add).then_inc(s["a_sum1"], 1)
                    else:
                        pool.wait_ge(s["a_sum1"], (NB - 1) * g + n - 1)
                        v.tensor_tensor(acc1[:], acc1[:], X[par][:, n, :], ALU.add).then_inc(s["a_sum1"], 1)

            def sum2(group, *js):
                g, par, _ = group
                for j in js:
                    pool.wait_ge(s["a_x2_rdy"], NB * g + j + 1)
                    if j == 0:
                        continue
                    if j == PART_MEAN and is_last(group):
                        pool.wait_ge(s["a_part_mean"], 1)
                    if j == 1:
                        if not is_first(group):
                            pool.wait_ge(s["a_mean2"], g)
                        v.tensor_tensor(acc2[:], X[par][:, 0, :], X[par][:, 1, :], ALU.add).then_inc(s["a_sum2"], 1)
                    else:
                        pool.wait_ge(s["a_sum2"], (NB - 1) * g + j - 1)
                        v.tensor_tensor(acc2[:], acc2[:], X[par][:, j, :], ALU.add).then_inc(s["a_sum2"], 1)

            def low(g, blocks):
                for a in blocks:
                    pool.wait_ge(s["a_hi_rdy"], NB * g + a + 1)
                    v.tensor_tensor(h_lo[:, a, :], H[:, a, :], h_hi[:, a, :], ALU.subtract
                                    ).then_inc(s["a_lo_rdy"], 1)

            def step(group):
                g, par, b = group
                sum2(group, *range(0, 6))
                if not is_last(group):
                    sum1(following(group), b + 2 if par == 1 else b + 1)
                sum2(group, *range(6, NB - 1))
                if not is_last(group):
                    low(g + 1, range(0, 8))
                sum2(group, NB - 1)
                if not is_last(group):
                    low(g + 1, range(8, NB))

            first = (0, 0, 0)
            sum1(first, 1)
            for r in range(SLICES):
                low(0, range(SLICE * r, SLICE * (r + 1)))
                if r == SLICES - 2:
                    sum1(following(first), 1)
                if r > 0:
                    sum2(first, *range(SLICE * (r - 1), SLICE * r))
            sum2(first, 12, 13, 14)
            low(1, range(0, 8))
            sum2(first, 15)
            low(1, range(8, NB))
            over_later_groups(pool, step)

        @block.scalar
        def _(act):
            def squares1(g, ns=range(NP2)):
                for n in ns:
                    act.wait_ge(s["a_dev1"], NP2 * g + n + 1)
                    if n >= 2:
                        act.wait_ge(s["a_sqa1"], (NB - 1) * g + 2 * (n - 2) + 1)
                    nc.scalar.activation(sq[:, n % 2], H[:, 2 * n:2 * n + 2, :], ACT.Square).then_inc(s["a_sq1_rdy"], 1)

            def squares2(g):
                for n in range(NP2):
                    act.wait_ge(s["a_dev2"], NP2 * g + n + 1)
                    nc.scalar.activation(sq[:, n % 2], sq[:, n % 2], ACT.Square).then_inc(s["a_sq2_rdy"], 1)

            def sigma(var_rdy, g, done, source=var):
                act.wait_ge(var_rdy, g + 1)
                nc.scalar.activation(sqa[:], source[:], ACT.Sqrt, bias=epsc[:, 0:1]).then_inc(done, 1)

            def high(g, a):
                act.wait_ge(s["a_h_rdy"], NB * g + a + 1)
                if not (isinstance(g, int) and g == 0):
                    if a < NB - 1:
                        act.wait_ge(s["a_hl_free"], (NB - 1) * (g - 1) + a + 1)
                    else:
                        act.wait_ge(s["a_conv_rdy"], NB * g)
                nc.scalar.activation(h_hi[:, a, :], H[:, a, :], ACT.Copy).then_inc(s["a_hi_rdy"], 1)

            def split(g, blocks, t):
                for n, a in enumerate(blocks):
                    act.wait_ge(s["a_u1"], NP2 * g + a // 2 + 1)
                    nc.scalar.activation(H[:, a, :], H[:, a, :], ACT.Identity, scale=t[:, CA * NB + a:CA * NB + a + 1],
                                         bias=t[:, SA * NB + a:SA * NB + a + 1]).then_inc(s["a_h_rdy"], 1)
                    if n:
                        high(g, a - 1)
                high(g, blocks[-1])

            def current(group):
                g, _, b = group
                nc.scalar.activation(now[:].rearrange("p m c -> p (m c)"), entry_of(modT, b, 0, 2 * NB), ACT.Copy
                                     ).then_inc(s["a_now_rdy"], 1)
                act.wait_ge(s["a_now_rdy"], g)

            def prepare(group):
                g = group[0]
                squares1(g)
                sigma(s["a_var1"], g, s["a_sd1"])
                current(group)
                split(g, range(NB), now[:].rearrange("p m c -> p (m c)"))

            def step(group):
                g = group[0]
                squares2(g - 1)
                sigma(s["a_var2"], g - 1, s["a_sd2"])
                if not is_last(group):
                    prepare(following(group))
                else:
                    bf_high(nc, act, L, F0, 0)
                    for d in range(2):
                        a_high(nc, act, L, F0, d)

            for dst, src in ((scal[:, 0:1], io["log_step"].to_broadcast([P, 1])), (st[:], io["state"]),
                             (trig[0:64], io["trig"][0].partition_broadcast(64)),
                             (trig[64:128], io["trig"][1].partition_broadcast(64)),
                             (vc[:], io["vcT"]), (bp[:], io["bp"]), (cospj[:], io["cos_pj"]), (idft[:], io["idft"]),
                             (dsb[:], io["dskip"]), (flip[:], io["flip"]), (unroll[:], io["unroll"])):
                act.dma_start(dst, src).then_inc(s["k_in"], 16)
            act.wait_ge(s["m_in"], 16 * NM_IN)
            nc.scalar.activation(ce[:], ct[:], ACT.Exp, scale=-1.0).then_inc(s["m_exp"], 1)
            act.wait_ge(s["k_zero_rdy"], 1)
            act.dma_start(io["kpad"][0:P].rearrange("(a b) -> a b", a=1), zero[:]).then_inc(s["k_out"], 16)
            act.wait_ge(s["k_in"], 16 * NK_IN)
            nc.scalar.activation(kt[2][:], trig[:, 0, :], ACT.Square, scale=st[:, 0:1]).then_inc(s["k_sq_rdy"], 1)
            act.wait_ge(s["k_den"], 1)
            nc.scalar.activation(kt[3][:], kt[1][:], ACT.Square).then_inc(s["k_sq2_rdy"], 1)
            squares1(0, range(0, 5))
            act.wait_ge(s["k_KT_sb"], 1)
            act.dma_start(io["kpad"][P:P + D].rearrange("(a b) -> a b", a=NB), KT[:]).then_inc(s["k_out"], 16)
            act.wait_ge(s["k_out"], 32)
            src = io["kpad"][1:P + D]
            toeplitz = bass.AP(tensor=src.tensor, offset=src.offset, ap=[[1, P], [1, D]])
            act.dma_start(strip[:], toeplitz).then_inc(s["k_strip_in"], 16)
            squares1(0, range(5, 8))
            act.wait_ge(s["k_strip_ps"], 1)
            nc.scalar.activation(S_hi[:], conv[:, 0:4, :].rearrange("p b r -> p (b r)"), ACT.Copy).then_inc(s["k_hi"], 1)
            sigma(s["a_var1"], 0, s["a_sd1"])
            act.wait_ge(s["k_S_rdy"], 1)
            for r in range(SLICES):
                act.wait_ge(s["m_slice_rdy"], r + 1)
                if r == SLICES - 1:
                    act.wait_ge(s["m_w_used"], NW1)
                split(0, range(SLICE * r, SLICE * (r + 1)), modT[:, 0, :])
            prepare((1, 1, 0))
            over_later_groups(act, step)
            squares2(NG - 1)
            sigma(s["a_var_rdy"], 0, s["a_sd2"], acc1)



def phases_f_b(nc, io, keep):
    modT, W_hi, W_lo = keep["modT"], keep["W_hi"], keep["W_lo"]
    with ExitStack() as ctx:
        sb = lambda n, s, d=F32: ctx.enter_context(nc.sbuf_tensor(n, s, d))
        base = keep["layer_base"]
        at = lambda n, kib, s, d=F32: nc.alloc_sbuf_tensor_at(n, s, d, offset=base + int(kib * KB))
        X2 = at("b_x2", 0, [P, NB, G])
        T = at("b_t", 32, [P, T_RING, G])
        h_hi = at("b_hi", 40, [P, HL_RING, G], F32R)
        h_lo = at("b_lo", 48, [P, HL_RING, G], F32R)
        stat = at("b_stat", 56, [P, GPB, 2, G])
        O = at("b_o", 64, [P, O_RING, G])
        now = sb("b_now", [P, GPB, (NMOD + 1 - SB) * NB])
        L, fw = keep["L"], keep["fw"]
        A_hi, A_lo, W = L["A_hi"], L["A_lo"], L["W"]
        ps = ctx.enter_context(nc.psum_tensor("l_ps", [P, BANKS, G], F32))

        def by_half(letter, names):
            return [{n: ctx.enter_context(nc.semaphore(f"{letter}{h}_{n}")) for n in names.split()} for h in range(2)]

        FS = [keep["F0"], fold_semaphores(nc, ctx, 1)]
        BS = by_half("b", "now_rdy early_in late_in dev u h_rdy hi_rdy lo_rdy hl_free ps_rdy gated out_rdy "
                          + " ".join(f"stored{n}" for n in range(O_RING))
                          + " " + " ".join(f"stat_in{n}" for n in range(GPB)))
        block = ctx.enter_context(nc.Block())

        feature = lambda half, k: (HB * (1 - half) + k) % NB
        place = lambda half, k: (NH * half + k) % NB
        FIRST = (0, 0, 0)

        @block.sync
        def _(sp):
            def load(half, group, k0, sem, n=NH):
                for k in range(k0, k0 + n, PART):
                    sp.dma_start(X2[:, place(half, k):place(half, k) + PART, :],
                                 of_group(io["x2"], group[0], feature(half, k), PART)).then_inc(sem, 16)

            def load_stat(half, group):
                g, par, _ = group
                sp.dma_start(stat[:, par], of_group(io["stat"], g, 0, 2)).then_inc(BS[half][f"stat_in{par}"], 16)

            def fold(half):
                S = FS[half]
                for d in range(NB):
                    if d >= A_RING:
                        load_a(sp, io, L, S, d)
                    if d == AT_LOAD:
                        sp.wait_ge(S["bf_lo_rdy"], ER)
                        if half > 0:
                            sp.wait_ge(BS[half - 1]["out_rdy"], HB * NG)
                        load_stat(half, FIRST)
                    for c in range(2):
                        n = 2 * d + c
                        if n >= W_RING:
                            sp.wait_ge(S["hi_rdy"], n - W_RING + 1)
                            sp.wait_ge(S["lo_rdy"], n - W_RING + 1)
                        elif half == 0:
                            continue
                        elif n < W_RING - O_RING:
                            sp.wait_ge(BS[half - 1]["ps_rdy"], HB * NG)
                        else:
                            sp.wait_ge(BS[half - 1][f"stored{n - (W_RING - O_RING)}"], 16 * NG * (HB // O_RING))
                        load_w(sp, io, L, S, half, n)
                    if 0 < d - AT_LOAD <= NH // PART:
                        load(half, FIRST, PART * (d - AT_LOAD - 1), BS[half]["early_in"], PART)
                sp.wait_ge(S["ps_rdy"], NT)
                load(half, FIRST, NH, BS[half]["late_in"])

            def step(half, group):
                g, S = group[0], BS[half]
                if not is_last(group):
                    sp.wait_ge(S["dev"], NB * g + NH)
                    load_stat(half, following(group))
                    load(half, following(group), 0, S["early_in"])
                elif half == 0:
                    sp.wait_ge(S["u"], NB * g)
                    load_bf_a(sp, io, L, FS[1], 1)
                for o in range(HB):
                    sp.wait_ge(S["out_rdy"], HB * g + o + 1)
                    sp.dma_start(of_group(io["out"], g, half * HB + o, 1), O[:, o % O_RING:o % O_RING + 1, :]
                                 ).then_inc(S[f"stored{o % O_RING}"], 16)
                if not is_last(group):
                    load(half, following(group), NH, S["late_in"])

            for half in range(2):
                fold(half)
                over_groups(sp, lambda group: step(half, group))
            for half in range(2):
                for n in range(O_RING):
                    sp.wait_ge(BS[half][f"stored{n}"], 16 * NG * (HB // O_RING))

        @block.vector
        def _(dve):
            v = nc.vector

            def fold(half):
                S = FS[half]
                for n in range(NT):
                    d, c = divmod(n, 2)
                    if n + 1 in AT_FIRST:
                        normalize(half, FIRST, [AT_FIRST.index(n + 1)])
                    dve.wait_ge(S["ps_rdy"], n + 1)
                    dve.wait_ge(S[f"W_in{n % W_RING}"], 16 * (n // W_RING + 1))
                    v.tensor_tensor(W[n % W_RING][:], W[n % W_RING][:], ps[:, n % BANKS, :],
                                    ALU.add).then_inc(S["sum_rdy"], 1)
                    if c == 1 and d + 2 < NB:
                        a_low(nc, dve, L, S, d + 2)

            def normalize(half, group, ks):
                g, par, b = group
                S = BS[half]
                loads = g // GPB + 1 if isinstance(g, int) else (b + 1)
                for k in ks:
                    n = NB * g + k
                    if k == 0:
                        dve.wait_ge(S[f"stat_in{par}"], 16 * loads)
                        dve.wait_ge(S["early_in"], 16 * (NH // PART) * (g + 1))
                        if is_first(group) and half > 0:
                            dve.wait_ge(BS[half - 1]["lo_rdy"], NB * NG)
                    if k == NH:
                        dve.wait_ge(S["late_in"], 16 * (NH // PART) * (g + 1))
                    if not (is_first(group) and k < T_RING):
                        dve.wait_ge(S["lo_rdy"], n - T_RING + 1)
                    elif k == AHEAD:
                        dve.wait_ge(FS[half]["lo_rdy"], NT)
                    t = T[:, k % T_RING, :]
                    v.tensor_tensor(t, X2[:, place(half, k), :], stat[:, par, 0, :], ALU.subtract).then_inc(S["dev"], 1)
                    dve.wait_ge(S["dev"], n + 1)
                    v.tensor_tensor(t, t, stat[:, par, 1, :], ALU.mult).then_inc(S["u"], 1)

            def step(half, group):
                S = BS[half]
                normalize(half, group, range(AHEAD, NB))
                if not is_last(group):
                    normalize(half, following(group), range(AHEAD))
                elif half == 0:
                    bf_low(nc, dve, L, FS[1], 1, fw)
                    dve.wait_ge(S["u"], NB * NG)
                    for d in range(2):
                        a_low(nc, dve, L, FS[1], d)
                for o in range(HB):
                    dve.wait_ge(S["gated"], HB * group[0] + o + 1)
                    v.tensor_tensor(O[:, o % O_RING, :], O[:, o % O_RING, :], X2[:, place(half, NH + o), :],
                                    ALU.add).then_inc(S["out_rdy"], 1)

            for half in range(2):
                fold(half)
                over_groups(dve, lambda group: step(half, group))

        @block.scalar
        def _(act):
            comp = lambda m: (m - SB) * NB

            def fold(half):
                S = FS[half]
                for n in range(NT):
                    d, c = divmod(n, 2)
                    if c == 0 and d >= 1 and d + 1 < NB:
                        a_high(nc, act, L, S, d + 1)
                    if n in AT_FIRST:
                        split(half, FIRST, [AT_FIRST.index(n)])
                    act.wait_ge(S["sum_rdy"], n + 1)
                    nc.scalar.activation(W_hi[:, d, c * G:(c + 1) * G], W[n % W_RING][:], ACT.Copy
                                         ).then_inc(S["hi_rdy"], 1)

            def modulate(half, group, k):
                g, par, b = group
                S = BS[half]
                if k == 0:
                    nc.scalar.activation(now[:, par, :], entry_of(modT, b, SB * NB, (NMOD + 1 - SB) * NB), ACT.Copy
                                         ).then_inc(S["now_rdy"], 1)
                    act.wait_ge(S["now_rdy"], g + 1)
                act.wait_ge(S["u"], NB * g + k + 1)
                t = T[:, k % T_RING, :]
                cb, sbias = comp(CB) + feature(half, k), comp(SB) + feature(half, k)
                nc.scalar.activation(t, t, ACT.Identity, scale=now[:, par, cb:cb + 1],
                                     bias=now[:, par, sbias:sbias + 1]).then_inc(S["h_rdy"], 1)

            def high(half, group, k):
                g, S = group[0], BS[half]
                act.wait_ge(S["h_rdy"], NB * g + k + 1)
                if k >= HL_RING:
                    act.wait_ge(S["hl_free"], (NB - 1) * g + k - HL_RING + 1)
                elif k < HL_RING - 1 and not is_first(group):
                    act.wait_ge(S["hl_free"], (NB - 1) * (g - 1) + NB + k - HL_RING + 1)
                elif not is_first(group):
                    act.wait_ge(S["ps_rdy"], HB * g)
                elif k == AHEAD:
                    act.wait_ge(FS[half]["lo_rdy"], NT)
                nc.scalar.activation(h_hi[:, k % HL_RING, :], T[:, k % T_RING, :], ACT.Copy).then_inc(S["hi_rdy"], 1)

            def split(half, group, ks):
                for k in ks:
                    modulate(half, group, k)
                    high(half, group, k)

            def gate(half, group, o):
                g, par, _ = group
                S = BS[half]
                blk = half * HB + o
                act.wait_ge(S["ps_rdy"], HB * g + o + 1)
                if not (is_first(group) and o < O_RING):
                    act.wait_ge(S[f"stored{o % O_RING}"], 16 * ((HB // O_RING) * g + o // O_RING))
                nc.scalar.activation(O[:, o % O_RING, :], ps[:, o, :], ACT.Identity,
                                     scale=now[:, par, comp(GB) + blk:comp(GB) + blk + 1],
                                     bias=now[:, par, comp(GBIAS) + blk:comp(GBIAS) + blk + 1]
                                     ).then_inc(S["gated"], 1)

            def step(half, group):
                split(half, group, range(AHEAD, NB))
                if not is_last(group):
                    split(half, following(group), range(AHEAD))
                elif half == 0:
                    bf_high(nc, act, L, FS[1], 1)
                    act.wait_ge(BS[half]["u"], NB * NG)
                    for d in range(2):
                        a_high(nc, act, L, FS[1], d)
                for o in range(HB):
                    gate(half, group, o)

            for half in range(2):
                fold(half)
                over_groups(act, lambda group: step(half, group))

        @block.gpsimd
        def _(pool):
            def fold(half):
                S = FS[half]
                for n in range(NT):
                    d, c = divmod(n, 2)
                    cols = slice(c * G, (c + 1) * G)
                    if n in AT_FIRST:
                        low(half, FIRST, [AT_FIRST.index(n)])
                    pool.wait_ge(S["hi_rdy"], n + 1)
                    nc.gpsimd.tensor_tensor(W_lo[:, d, cols], W[n % W_RING][:], W_hi[:, d, cols],
                                            ALU.subtract).then_inc(S["lo_rdy"], 1)

            def low(half, group, ks):
                S = BS[half]
                for k in ks:
                    pool.wait_ge(S["hi_rdy"], NB * group[0] + k + 1)
                    nc.gpsimd.tensor_tensor(h_lo[:, k % HL_RING, :], T[:, k % T_RING, :], h_hi[:, k % HL_RING, :],
                                            ALU.subtract).then_inc(S["lo_rdy"], 1)

            def step(half, group):
                low(half, group, range(AHEAD, NB))
                if not is_last(group):
                    low(half, following(group), range(AHEAD))

            for half in range(2):
                fold(half)
                over_groups(pool, lambda group: step(half, group))

        @block.tensor
        def _(pe):
            mm = nc.tensor.matmul

            def fold(half):
                S = FS[half]
                pe.wait_ge(S["bf_hi_rdy"], ER)
                pe.wait_ge(S["bf_lo_rdy"], ER)
                for n in range(NT):
                    d, c = divmod(n, 2)
                    if c == 0:
                        pe.wait_ge(S["A_hi_rdy"], d + 1)
                        pe.wait_ge(S["A_lo_rdy"], d + 1)
                    if n >= BANKS:
                        pe.wait_ge(S["sum_rdy"], n - BANKS + 1)
                    elif half > 0:
                        pe.wait_ge(BS[half - 1]["gated"], HB * (NG - 1) + n + 1)
                    out = ps[:, n % BANKS, :]
                    cols = slice(c * G, (c + 1) * G)
                    hi, lo = L["bf_hi"][half], L["bf_lo"][half]
                    for e in range(ER):
                        mm(out, A_hi[:, d % 2, e, :], hi[:, e, cols], start=(e == 0), stop=False)
                        mm(out, A_hi[:, d % 2, e, :], lo[:, e, cols], start=False, stop=False)
                        last = mm(out, A_lo[:, d % 2, e, :], hi[:, e, cols], start=False, stop=(e == ER - 1))
                    last.then_inc(S["ps_rdy"], 1)

            def step(half, group):
                g, S = group[0], BS[half]
                for k in range(NB):
                    if is_first(group):
                        pe.wait_ge(FS[half]["lo_rdy"], 2 * (feature(half, k) + 1))
                    pe.wait_ge(S["hi_rdy"], NB * g + k + 1)
                    pe.wait_ge(S["lo_rdy"], NB * g + k + 1)
                    hi, lo = h_hi[:, k % HL_RING, :], h_lo[:, k % HL_RING, :]
                    for o in range(HB):
                        if k == 0:
                            if is_first(group):
                                pe.wait_ge(FS[half]["sum_rdy"], NT - BANKS + o + 1)
                            else:
                                pe.wait_ge(S["gated"], HB * (g - 1) + o + 1)
                        cols = slice(o * P, (o + 1) * P)
                        w_hi, w_lo = W_hi[:, feature(half, k), cols], W_lo[:, feature(half, k), cols]
                        mm(ps[:, o, :], w_hi, hi, start=(k == 0), stop=False)
                        mm(ps[:, o, :], w_hi, lo, start=False, stop=False)
                        last = mm(ps[:, o, :], w_lo, hi, start=False, stop=(k == NB - 1))
                        if k == NB - 1:
                            last.then_inc(S["ps_rdy"], 1)
                    if k < NB - 1:
                        last.then_inc(S["hl_free"], 1)

            for half in range(2):
                fold(half)
                over_groups(pe, lambda group: step(half, group))




def build(nc, io):
    with ExitStack() as top:
        sb = lambda ctx, n, s, d=F32: ctx.enter_context(nc.sbuf_tensor(n, s, d))
        keep = {
            "modT": sb(top, "modT", [P, BATCH, (NMOD + 1) * NB]),
            "ones": sb(top, "ones", [P, P]),
            "eps": sb(top, "eps", [P, 1]),
            "fw": sb(top, "f_weights", [P, 4, ER]),
            "F0": fold_semaphores(nc, top, 0),
        }
        keep["layer_base"] = nc.sbuf_base
        keep["L"] = fold_arrays(nc, nc.sbuf_base)
        with ExitStack() as conv:
            keep["S_hi"] = sb(conv, "S_hi", [P, D], F32R)
            keep["S_lo"] = sb(conv, "S_lo", [P, D], F32R)
            phase_a(nc, io, keep)
        with ExitStack() as layer:
            sb(layer, "l_slab", [P, 76 * KB // 4])
            keep["W_hi"] = sb(layer, "W_hi", [P, NB, HALF], F32R)
            keep["W_lo"] = sb(layer, "W_lo", [P, NB, HALF], F32R)
            phases_f_b(nc, io, keep)


def shape_tables():
    l = np.arange(D)
    theta = np.pi * l / D
    trig = np.stack([np.cos(theta), np.sin(theta)])
    trig[0, D // 2] = 0.0
    p, j, t1 = np.arange(P), np.arange(NB), np.arange(NB)
    t2 = np.arange(P)
    a = 2 * np.pi * np.outer(p, t2) / P + np.pi * p[:, None] / P
    u = (2 * np.pi * j[None, None, :] * t2[:, None, None] / D + np.pi * j[None, None, :] / D
         + 2 * np.pi * j[None, None, :] * t1[None, :, None] / NB)
    unroll = np.stack([np.cos(u), -np.sin(u)], axis=-1) / D
    return {
        "trig": trig.reshape(2, 2, D // 2).transpose(1, 0, 2),
        "cos_pj": trig[0].reshape(P, NB),
        "idft": np.stack([np.cos(a), np.sin(a)], axis=1),
        "unroll": unroll.reshape(P, NB, 2 * NB),
        "ident": np.eye(P),
        "flip": np.eye(P)[::-1],
        "ones": np.full((P, P), 1.0 / D),
        "eps": np.full((P, 1), EPS),
    }


def kernel(**inputs):
    import concourse.bacc as bacc
    from concourse.bass_utils import run_bass_kernel_spmd

    A = {k.removeprefix("L0_"): np.asarray(v) for k, v in inputs.items()}
    twice = lambda a: np.concatenate([a, a], axis=0)
    state = np.concatenate([A["attn_Lambda_ri"], A["attn_p_ri"], A["attn_q_ri"],
                            A["attn_Ct_ri"].reshape(N_STATE, 2)], axis=1)
    per_row = lambda a: np.repeat(a, NE // a.shape[0]).reshape(ER, P).T
    arrays = {
        "x": A["attn_u"].reshape(NG, G, NB, P).transpose(0, 3, 2, 1),
        "state": twice(state),
        "vcT": np.concatenate([A["attn_Vc_ri"].transpose(1, 2, 0)] * 2, axis=2),
        "bp": A["attn_Bp"],
        "dskip": A["attn_D"].reshape(1, 1),
        "log_step": A["attn_log_step"].reshape(1, 1),
        "cT": A["c"].T.reshape(NB, P, BATCH).transpose(1, 0, 2),
        "wmod1": A["wmod"][:, :3 * D].reshape(NB, P, 3, SLICES, SW).transpose(2, 3, 0, 1, 4),
        "wmod2": A["wmod"][:, 3 * D:].reshape(NB, P, 6, W2_COLS).transpose(2, 0, 1, 3),
        "biasT": A["ffn_bias"].reshape(NB, P).T,
        "W": A["ffn_W"].T.reshape(NB, P, 2, HALF).transpose(2, 0, 1, 3),
        "A": A["ffn_A"].reshape(ER, P, NB, P).transpose(1, 2, 0, 3),
        "bf": A["ffn_Bf"].transpose(0, 2, 1).reshape(ER, P, 2, HALF).transpose(2, 1, 0, 3),
        "wsc": np.stack([per_row(A["ffn_coeffs"]), per_row(A["ffn_scales"])], axis=1),
    }
    arrays.update({n: t.astype(np.float32) for n, t in shape_tables().items()})
    arrays = {n: np.ascontiguousarray(a) for n, a in arrays.items()}

    nc = bacc.Bacc("TRN2", target_bir_lowering=False, num_devices=1)
    io = {n: nc.dram_tensor(f"in_{n}", a.shape, F32, kind="ExternalInput").ap() for n, a in arrays.items()}
    io["out"] = nc.dram_tensor("out", (NG, P, NB, G), F32, kind="ExternalOutput").ap()
    io["x2"] = nc.dram_tensor("x2_scratch", (NG, P, NB, G), F32).ap()
    io["stat"] = nc.dram_tensor("stat_scratch", (NG, P, 2, G), F32).ap()
    io["kpad"] = nc.dram_tensor("k_scratch", (P + D,), F32).ap()
    build(nc, io)
    r = run_bass_kernel_spmd(nc, [{f"in_{n}": a for n, a in arrays.items()}], core_ids=[0])
    out = r.results[0]["out"]
    return np.ascontiguousarray(out.transpose(0, 3, 2, 1)).reshape(BATCH, ROWS // BATCH, D)
```
